# Optimizing a Trainium2 kernel written in Bass

```python
import numpy as np
import jax
import jax.numpy as jnp

def _softmax(x, axis=-1):
    return jax.nn.softmax(x, axis=axis)

def _gelu(x):
    return jax.nn.gelu(x, approximate=True)

def _silu(x):
    return jax.nn.silu(x)

def _sigmoid(x):
    return jax.nn.sigmoid(x)

def _layernorm(x, axis=-1, eps=1e-05):
    m = jnp.mean(x, axis=axis, keepdims=True)
    v = jnp.var(x, axis=axis, keepdims=True)
    return (x - m) / jnp.sqrt(v + eps)

def _scatter_add(tgt, idx, src, axis=0):
    return tgt.at[idx].add(src)

def _segment_sum(src, seg, n):
    return jax.ops.segment_sum(src, seg, n)
kernel_name = 'mk_flamingo_gated_d1_seqx_r8_f94d82'

def setup_inputs(seed: int=0):
    np.random.seed(seed)
    _w = jnp.asarray

    def _rec_inputs():
        import jax
        import jax.numpy as jnp
        _rk = jax.random.key(seed)
        x = 4.136e-05 + 0.9999 * jax.random.normal(jax.random.fold_in(_rk, 1), (64, 128, 128), jnp.float32)
        _lenS = 128 - jax.random.randint(jax.random.fold_in(_rk, 7), (64,), 0, max(1, 128 // 4) + 1, jnp.int32)
        _lenS2 = 77 - jax.random.randint(jax.random.fold_in(_rk, 8), (64,), 0, max(1, 77 // 4) + 1, jnp.int32)
        _ctx_1024P = jax.random.normal(jax.random.fold_in(_rk, 11), (64, 16, 128), jnp.float32)
        _ctx_1024c = jax.random.dirichlet(jax.random.fold_in(_rk, 511), 0.3 * jnp.ones((16,), jnp.float32), (64, 77))
        _ctx_1024t = jnp.einsum('bsk,bkd->bsd', _ctx_1024c, _ctx_1024P)
        _ctx_1024t = _ctx_1024t * jax.lax.rsqrt(jnp.mean(jnp.square(_ctx_1024t)) + 1e-12) * 0.953939
        ctx_1024 = -0.000125008 + 0.999885 * (_ctx_1024t + 0.3 * jax.random.normal(jax.random.fold_in(_rk, 611), (64, 77, 128), jnp.float32))
        _g = jax.random.normal(jax.random.fold_in(_rk, 9001), (2, 1), jnp.float32)
        _g = jnp.sign(_g) * jnp.maximum(jnp.abs(_g), 1.0) + (_g == 0) * 1.0
        g_xattn = _g[0]
        g_ffn = _g[1]
        return (x, ctx_1024, g_xattn, g_ffn)
    x, ctx_1024, g_xattn, g_ffn = _rec_inputs()

    def _L0_xattn_setup():
        import jax, jax.numpy as jnp
        import numpy as np
        EMB = 128
        key = jax.random.key(seed)
        k1, k2, k3, k4, k5 = jax.random.split(key, 5)
        batch = jax.random.normal(k1, (8, 512, EMB), dtype=jnp.float32)
        latent = jax.random.normal(k2, (8, 128, EMB), dtype=jnp.float32)
        s = 1.0 / np.sqrt(EMB)
        Wk = jax.random.normal(k3, (EMB, EMB), dtype=jnp.float32) * s
        Wq = jax.random.normal(k4, (EMB, EMB), dtype=jnp.float32) * s
        Wv = jax.random.normal(k5, (EMB, EMB), dtype=jnp.float32) * s
        return {'batch': batch, 'latent': latent, 'Wk': Wk, 'Wq': Wq, 'Wv': Wv}
    _L0_xattn_all = _L0_xattn_setup()
    _L0_xattn_in = {k: v for k, v in _L0_xattn_all.items() if k in ('Wk', 'Wq', 'Wv')}
    del _L0_xattn_all

    def _L0_ffn_setup():
        import jax, jax.numpy as jnp
        import numpy as np
        B, T, C, H, E, MIN_E = (4, 256, 128, 128, 16, 2)
        IS_CAUSAL = False

        def _forward(hidden_states, sim_matrix, gates, q_proj, k_proj, v_proj, o_proj):
            b, t, c = hidden_states.shape
            n = b * t
            x = hidden_states.reshape(n, c)
            xn = x / jnp.maximum(jnp.linalg.norm(x, axis=-1, keepdims=True), 1e-12)
            sn = sim_matrix / jnp.maximum(jnp.linalg.norm(sim_matrix, axis=0, keepdims=True), 1e-12)
            logits = xn @ sn - jax.nn.sigmoid(gates)
            gated = jax.nn.relu(logits)
            hard = (gated > 0).astype(gated.dtype)
            mask = gated + jax.lax.stop_gradient(hard - gated)
            inactive = jnp.sum(hard, axis=1) == 0
            _, fb_idx = jax.lax.top_k(logits, MIN_E)
            fb = jnp.zeros((n, logits.shape[1]), gated.dtype).at[jnp.arange(n)[:, None], fb_idx].set(1.0)
            put = jax.lax.stop_gradient(inactive[:, None].astype(gated.dtype) * fb)
            mask = mask * (1.0 - put) + put
            masked = jnp.where(mask > 0, gated, -jnp.inf)
            w = jax.nn.softmax(masked, axis=-1)

            def moe_proj(p):
                y = jnp.einsum('nc,ech->neh', x, p)
                return jnp.einsum('ne,neh->nh', w, y)
            q = moe_proj(q_proj).reshape(b, t, -1)
            k = moe_proj(k_proj).reshape(b, t, -1)
            v = moe_proj(v_proj).reshape(b, t, -1)
            h = q.shape[-1]
            scores = jnp.einsum('bth,bsh->bts', q, k) / jnp.sqrt(jnp.asarray(h, q.dtype))
            if IS_CAUSAL and t > 1:
                causal = jnp.tril(jnp.ones((t, t), bool))
                scores = jnp.where(causal[None], scores, -jnp.inf)
            attn = jax.nn.softmax(scores, axis=-1)
            o = jnp.einsum('bts,bsh->bth', attn, v).reshape(n, h)
            z = jnp.einsum('ne,nh->enh', w, o)
            out = jnp.einsum('enh,ehc->nc', z, o_proj)
            return out.reshape(b, t, c)
        key = jax.random.key(seed)
        ks = jax.random.split(key, 6)
        lim_qkv = float(np.sqrt(6.0 / (C + H)))
        inp = {'hidden_states': jax.random.normal(ks[0], (B, T, C), jnp.float32), 'sim_matrix': jax.random.normal(ks[1], (C, E), jnp.float32), 'gates': jnp.zeros((E,), jnp.float32), 'q_proj': jax.random.uniform(ks[2], (E, C, H), jnp.float32, -lim_qkv, lim_qkv), 'k_proj': jax.random.uniform(ks[3], (E, C, H), jnp.float32, -lim_qkv, lim_qkv), 'v_proj': jax.random.uniform(ks[4], (E, C, H), jnp.float32, -lim_qkv, lim_qkv), 'o_proj': jax.random.uniform(ks[5], (E, H, C), jnp.float32, -lim_qkv, lim_qkv)}
        return inp
    _L0_ffn_all = _L0_ffn_setup()
    _L0_ffn_in = {k: v for k, v in _L0_ffn_all.items() if k in ('sim_matrix', 'gates', 'q_proj', 'k_proj', 'v_proj', 'o_proj')}
    del _L0_ffn_all
    return {'x': x, 'ctx_1024': ctx_1024, 'g_xattn': g_xattn, 'g_ffn': g_ffn, 'L0_xattn_Wk': _L0_xattn_in['Wk'], 'L0_xattn_Wq': _L0_xattn_in['Wq'], 'L0_xattn_Wv': _L0_xattn_in['Wv'], 'L0_ffn_sim_matrix': _L0_ffn_in['sim_matrix'], 'L0_ffn_gates': _L0_ffn_in['gates'], 'L0_ffn_q_proj': _L0_ffn_in['q_proj'], 'L0_ffn_k_proj': _L0_ffn_in['k_proj'], 'L0_ffn_v_proj': _L0_ffn_in['v_proj'], 'L0_ffn_o_proj': _L0_ffn_in['o_proj']}

def reference(x, ctx_1024, g_xattn, g_ffn, L0_xattn_Wk, L0_xattn_Wq, L0_xattn_Wv, L0_ffn_sim_matrix, L0_ffn_gates, L0_ffn_q_proj, L0_ffn_k_proj, L0_ffn_v_proj, L0_ffn_o_proj):
    import jax
    import jax.numpy as jnp

    def _L0_xattn_ref(batch, latent, Wk, Wq, Wv):
        import jax, jax.numpy as jnp
        import numpy as np
        EMB = 128
        keys = jnp.einsum('bpe,fe->bpf', batch, Wk)
        queries = jnp.einsum('ble,fe->blf', latent, Wq)
        values = jnp.einsum('bpe,fe->bpf', batch, Wv)
        scale = 1.0 / jnp.sqrt(jnp.asarray(batch.shape[-1], dtype=batch.dtype))
        weights = jnp.einsum('ble,bpe->blp', queries, keys) * scale
        weights = jax.nn.softmax(weights, axis=-1)
        attention = jnp.einsum('blp,bpe->ble', weights, values)
        return attention

    def _L0_ffn_ref(hidden_states, sim_matrix, gates, q_proj, k_proj, v_proj, o_proj):
        import jax, jax.numpy as jnp
        import numpy as np
        B, T, C, H, E, MIN_E = (4, 256, 128, 128, 16, 2)
        IS_CAUSAL = False

        def _forward(hidden_states, sim_matrix, gates, q_proj, k_proj, v_proj, o_proj):
            b, t, c = hidden_states.shape
            n = b * t
            x = hidden_states.reshape(n, c)
            xn = x / jnp.maximum(jnp.linalg.norm(x, axis=-1, keepdims=True), 1e-12)
            sn = sim_matrix / jnp.maximum(jnp.linalg.norm(sim_matrix, axis=0, keepdims=True), 1e-12)
            logits = xn @ sn - jax.nn.sigmoid(gates)
            gated = jax.nn.relu(logits)
            hard = (gated > 0).astype(gated.dtype)
            mask = gated + jax.lax.stop_gradient(hard - gated)
            inactive = jnp.sum(hard, axis=1) == 0
            _, fb_idx = jax.lax.top_k(logits, MIN_E)
            fb = jnp.zeros((n, logits.shape[1]), gated.dtype).at[jnp.arange(n)[:, None], fb_idx].set(1.0)
            put = jax.lax.stop_gradient(inactive[:, None].astype(gated.dtype) * fb)
            mask = mask * (1.0 - put) + put
            masked = jnp.where(mask > 0, gated, -jnp.inf)
            w = jax.nn.softmax(masked, axis=-1)

            def moe_proj(p):
                y = jnp.einsum('nc,ech->neh', x, p)
                return jnp.einsum('ne,neh->nh', w, y)
            q = moe_proj(q_proj).reshape(b, t, -1)
            k = moe_proj(k_proj).reshape(b, t, -1)
            v = moe_proj(v_proj).reshape(b, t, -1)
            h = q.shape[-1]
            scores = jnp.einsum('bth,bsh->bts', q, k) / jnp.sqrt(jnp.asarray(h, q.dtype))
            if IS_CAUSAL and t > 1:
                causal = jnp.tril(jnp.ones((t, t), bool))
                scores = jnp.where(causal[None], scores, -jnp.inf)
            attn = jax.nn.softmax(scores, axis=-1)
            o = jnp.einsum('bts,bsh->bth', attn, v).reshape(n, h)
            z = jnp.einsum('ne,nh->enh', w, o)
            out = jnp.einsum('enh,ehc->nc', z, o_proj)
            return out.reshape(b, t, c)
        return _forward(hidden_states, sim_matrix, gates, q_proj, k_proj, v_proj, o_proj)
    x = x + jnp.tanh(g_xattn[0]) * _L0_xattn_ref(ctx_1024, _layernorm(x, axis=-1), L0_xattn_Wk, L0_xattn_Wq, L0_xattn_Wv)
    x = x + jnp.tanh(g_ffn[0]) * _L0_ffn_ref(_layernorm(x, axis=-1), L0_ffn_sim_matrix, L0_ffn_gates, L0_ffn_q_proj, L0_ffn_k_proj, L0_ffn_v_proj, L0_ffn_o_proj)
    return x

_drawn_inputs = setup_inputs


def setup_inputs(seed=0):
    import zlib

    import numpy as np

    out = dict(_drawn_inputs(seed))
    spreads = {'L0_ffn_gates': (0.0, 0.1)}
    factors = {}
    for name, (base, spread) in spreads.items():
        noise = np.random.default_rng([zlib.crc32(name.encode()), seed]).standard_normal(out[name].shape)
        drawn = base * np.exp(spread * noise) if base else spread * noise
        out[name] = jnp.asarray(drawn.astype(out[name].dtype))
    for name, factor in factors.items():
        out[name] = (out[name] * factor).astype(out[name].dtype)
    return out
```

```python
from contextlib import ExitStack

import concourse.bass as bass
from concourse import mybir

ALU = mybir.AluOpType
ACT = mybir.ActivationFunctionType
F32 = mybir.dt.float32
F16 = mybir.dt.float16
U32 = mybir.dt.uint32
I32 = mybir.dt.int32
AX_X = mybir.AxisListType.X
ABSMAX = bass.bass_isa.ReduceOp.absmax

P = 128
G = 4
Q, K, V, O = range(4)
EPS = 1e-5
X_UP = 4096.0
W_UP = 16384.0
Z_SLOTS = 4
GATE_STEPS = 13
EXP_AT = 8


def flamingo_gated_moe_attention(nc, x, ctx_in, g_xattn, g_ffn, Wk, Wq, Wv, sim_matrix, gates,
                                 q_proj, k_proj, v_proj, o_proj, out):
    B, T, C = x.shape
    _, S, _ = ctx_in.shape
    E = sim_matrix.shape[1]
    assert T == P and C == P and E == 16 and B % G == 0
    NG = B // G
    N = G * P
    LOOP = (3, NG - 2)
    CHUNK = B // 4
    RSQRT_C = float(P) ** -0.5

    with ExitStack() as ctx:
        def sb(name, shape, dt=F32):
            return ctx.enter_context(nc.sbuf_tensor(name, shape, dt))

        def psum(name):
            return ctx.enter_context(nc.psum_tensor(name, [P, N], F32))

        def sem(name):
            return ctx.enter_context(nc.semaphore(name))

        x_all = sb("x_all", [P, B, C])
        ctx_g = sb("ctx_g", [S, G, C])
        w_hi = sb("w_hi", [P, 4, E, P], F16)
        w_lo = sb("w_lo", [P, 4, E, P], F16)
        w_all = sb("w_all", [P, B, E])
        z = sb("z", [P, 2, E, N], F16)
        stage = z[:].rearrange("p a e n -> p (a e n)").bitcast(F32).rearrange("p (m e h) -> p m e h", m=4, e=E)
        z_full = sb("z_full", [P, Z_SLOTS, N])
        ident = sb("ident", [P, P])
        ident16 = sb("ident16", [P, P], F16)
        ones = sb("ones", [P, P])
        sel = sb("sel", [2 * E, E, P], F16)
        iota_i = sb("iota_i", [P, E], I32)
        iota_f = sb("iota_f", [P, E])
        minus_half = sb("minus_half", [P, G])
        plus_half = sb("plus_half", [P, E])
        gx = sb("gx", [P, 1])
        gf = sb("gf", [P, 1])
        tanh_x = sb("tanh_x", [P, 1])
        tanh_f = sb("tanh_f", [P, 1])
        gates_b = sb("gates_b", [P, E])
        sig = sb("sig", [P, E])
        sim_sb = sb("sim_sb", [P, E])
        sim_sq = sb("sim_sq", [P, E])
        sim_nrm = sb("sim_nrm", [P, E])
        sn = sb("sn", [P, E])
        wk_sb = sb("wk_sb", [P, P])
        wq_sb = sb("wq_sb", [P, P])
        wv_sb = sb("wv_sb", [P, P])
        m_qk = sb("m_qk", [P, P])
        wvT = sb("wvT", [P, P])
        wmax = sb("wmax", [P, 4])
        wmax_all = sb("wmax_all", [P, 4])
        w_pow = sb("w_pow", [P, 4])
        w_up = sb("w_up", [P, 4])
        score_scale = sb("score_scale", [P, 1])
        out_scale = sb("out_scale", [P, 1])
        bn1 = sb("bn1", [P, G, 6])
        mv1 = sb("mv1", [P, G, 2])
        rstd1 = sb("rstd1", [P, G])
        xn = sb("xn", [P, G, C])
        xnT = sb("xnT", [P, N])
        qxT = sb("qxT", [P, N])
        ctxT = sb("ctxT", [P, G * S])
        nmax_x = sb("nmax_x", [P, G])
        px = sb("px", [P, G, S])
        sum_x = sb("sum_x", [P, G])
        rsum_x = sb("rsum_x", [P, G])
        pxT = sb("pxT", [S, N])
        vx = sb("vx", [S, N])
        bn2 = sb("bn2", [P, G, 6])
        mv2 = sb("mv2", [P, G, 2])
        rstd2 = sb("rstd2", [P, G])
        norm2 = sb("norm2", [P, G])
        rnorm2 = sb("rnorm2", [P, G])
        x2 = sb("x2", [P, G, C])
        x2T = sb("x2T", [P, N])
        logit = sb("logit", [P, G, E])
        top = sb("top", [P, G, 8])
        top_at = sb("top_at", [P, G, 8], U32)
        gate_max = sb("gate_max", [P, G])
        inactive = sb("inactive", [P, G])
        gate_arg = sb("gate_arg", [P, G, E])
        gate_e = sb("gate_e", [P, G, E])
        fb0 = sb("fb0", [P, G, E])
        fb1 = sb("fb1", [P, G, E])
        mask = sb("mask", [P, G, E])
        wsum = sb("wsum", [P, G])
        w_split = sb("w_split", [P, G, 2 * E], F16)
        w_splitT = sb("w_splitT", [2 * E, N], F16)
        qT = sb("qT", [P, N])
        kT = sb("kT", [P, N])
        vT = sb("vT", [P, N])
        v_sb = sb("v_sb", [P, G, P])
        nmax_c = sb("nmax_c", [P, G])
        pc = sb("pc", [P, G, P])
        sum_c = sb("sum_c", [P, G])
        rsum_c = sb("rsum_c", [P, G])
        rs_c = sb("rs_c", [P, G])
        pcT = sb("pcT", [P, N])
        o_hi = sb("o_hi", [P, N], F16)
        o_lo = sb("o_lo", [P, N], F16)
        w_out = sb("w_out", [P, G, E])
        acc_p = [psum("acc_q"), psum("acc_k"), psum("acc_v")]
        wb_p = [psum("wb0"), psum("wb1")]
        y_p = psum("y")
        m0 = psum("m0")
        m1 = psum("m1")

        x_in = [sem(f"x_in{c}") for c in range(4)]
        ctx_loaded = sem("ctx_loaded")
        small_in = sem("small_in")
        proj_in = [sem(f"proj_in{m}") for m in range(4)]
        out_stored = sem("out_stored")
        pool_set = sem("pool_set")
        consts = sem("consts")
        passed = sem("passed")
        tanh_done = sem("tanh_done")
        prep_pe = sem("prep_pe")
        prep_dve = sem("prep_dve")
        prep_chain = sem("prep_chain")
        wmax_done = sem("wmax_done")
        wmax_shared = sem("wmax_shared")
        hi_done = sem("hi_done")
        lo_done = sem("lo_done")
        nrm_root = sem("nrm_root")
        bn1_done = sem("bn1_done")
        rstd1_done = sem("rstd1_done")
        xn_done = sem("xn_done")
        xnT_ps = sem("xnT_ps")
        xnT_sb = sem("xnT_sb")
        qxT_ps = sem("qxT_ps")
        qxT_sb = sem("qxT_sb")
        ctxT_ps = sem("ctxT_ps")
        ctxT_sb = sem("ctxT_sb")
        xscore_ps = sem("xscore_ps")
        xmax_done = sem("xmax_done")
        xexp_done = sem("xexp_done")
        vx_ps = sem("vx_ps")
        vx_sb = sem("vx_sb")
        pxT_ps = sem("pxT_ps")
        pxT_sb = sem("pxT_sb")
        att_ps = sem("att_ps")
        rsum_x_done = sem("rsum_x_done")
        x1_done = sem("x1_done")
        bn2_done = sem("bn2_done")
        rstd2_done = sem("rstd2_done")
        norm_step = sem("norm_step")
        rnorm_done = sem("rnorm_done")
        rnorm_inv = sem("rnorm_inv")
        x2_done = sem("x2_done")
        x2T_ps = sem("x2T_ps")
        x2T_sb = sem("x2T_sb")
        logit_ps = sem("logit_ps")
        gate_step = sem("gate_step")
        gate_arg_done = sem("gate_arg_done")
        gate_exp = sem("gate_exp")
        w_ready = sem("w_ready")
        wT_ps = sem("wT_ps")
        wT_sb = sem("wT_sb")
        wb_ps = sem("wb_ps")
        z_full_done = sem("z_full_done")
        z_hi_done = sem("z_hi_done")
        z_lo_done = sem("z_lo_done")
        expert_used = sem("expert_used")
        acc_ps = [sem("q_ps"), sem("k_ps"), sem("v_ps")]
        acc_sb = [sem("q_sb"), sem("k_sb"), sem("vT_sb")]
        v_ps = sem("v_tok_ps")
        v_tok_sb = sem("v_tok_sb")
        cscore_ps = sem("cscore_ps")
        cmax_done = sem("cmax_done")
        cexp_done = sem("cexp_done")
        cpT_ps = sem("cpT_ps")
        cpT_sb = sem("cpT_sb")
        oT_ps = sem("oT_ps")
        o_hi_done = sem("o_hi_done")
        o_lo_done = sem("o_lo_done")
        rsum_c_done = sem("rsum_c_done")
        rs_c_done = sem("rs_c_done")
        w_out_done = sem("w_out_done")
        y_ps = sem("y_ps")
        y_added = sem("y_added")

        block = ctx.enter_context(nc.Block())

        def wait(eng, s, count):
            if not isinstance(count, int) or count > 0:
                eng.wait_ge(s, count)

        def plain(eng):
            eng.sem_inc(passed, 1)

        def cap(groups):
            return min(groups, NG) if isinstance(groups, int) else groups

        def has(g):
            return not isinstance(g, int) or 0 <= g < NG

        def passes(eng, body, loads=()):
            for i in range(-2, LOOP[0]):
                body(i)
            for load in loads:
                eng.wait_ge(load, 16)
            with eng.Fori(LOOP[0], LOOP[1]) as i:
                body(i)
            for i in range(LOOP[1], NG + 2):
                body(i)

        def rows(t, g, b):
            return t[:, bass.ds(G * g + b, 1), :].rearrange("p a c -> p (a c)")

        def tok(b):
            return slice(b * P, (b + 1) * P)

        @block.sync
        def _(sp):
            x_v = x.rearrange("b n c -> n b c")
            c_v = ctx_in.rearrange("b s c -> s b c")
            sp.dma_start(x_all[:, 0:CHUNK, :], x_v[:, 0:CHUNK, :]).then_inc(x_in[0], 16)
            for dst, src in ((wq_sb, Wq), (wk_sb, Wk), (wv_sb, Wv), (sim_sb, sim_matrix)):
                sp.dma_start(dst[:], src).then_inc(small_in, 16)
            sp.dma_start(gx[:], g_xattn.partition_broadcast(P)).then_inc(small_in, 16)
            sp.dma_start(gf[:], g_ffn.partition_broadcast(P)).then_inc(small_in, 16)
            sp.dma_start(gates_b[:], gates.partition_broadcast(P)).then_inc(small_in, 16)
            sp.dma_start(ctx_g[:], c_v[:, 0:G, :]).then_inc(ctx_loaded, 16)
            for m, w in enumerate((q_proj, k_proj, v_proj, o_proj)):
                sp.dma_start(stage[:, m], w.rearrange("e c h -> c e h")).then_inc(proj_in[m], 16)
            for c in range(1, 4):
                sp.dma_start(x_all[:, c * CHUNK:(c + 1) * CHUNK, :],
                             x_v[:, c * CHUNK:(c + 1) * CHUNK, :]).then_inc(x_in[c], 16)
            o_v = out.rearrange("b n c -> n b c")

            def load_context(g):
                sp.wait_ge(ctxT_ps, g)
                sp.dma_start(ctx_g[:], c_v[:, bass.ds(G * g, G), :]).then_inc(ctx_loaded, 16)

            def store(g):
                sp.wait_ge(y_added, G * E * g + G * E)
                sp.dma_start(o_v[:, bass.ds(G * g, G), :], x_all[:, bass.ds(G * g, G), :]).then_inc(out_stored, 16)

            for g in range(1, 5):
                load_context(g)
            with sp.Fori(5, NG) as g:
                load_context(g)
                store(g - 5)
            for g in range(NG - 5, NG):
                store(g)
            sp.wait_ge(out_stored, 16 * NG)

        @block.gpsimd
        def _(pool):
            nc.gpsimd.memset(ident[:], 0.0).then_inc(pool_set, 1)
            nc.gpsimd.memset(ident16[:], 0.0).then_inc(pool_set, 1)
            nc.gpsimd.memset(sel[:], 0.0).then_inc(pool_set, 1)
            nc.gpsimd.memset(ones[:], 1.0)
            nc.gpsimd.memset(minus_half[:], -0.5)
            nc.gpsimd.memset(plus_half[:], 0.5)
            nc.gpsimd.iota(iota_i[:], pattern=[[1, E]], base=0, channel_multiplier=0).then_inc(pool_set, 1)
            pool.wait_ge(pool_set, 4)
            for m in (ident, ident16):
                nc.gpsimd.affine_select(out=m[:], in_=m[:], compare_op=ALU.not_equal, fill=1.0, base=0,
                                        pattern=[[-1, P]], channel_multiplier=1)
            nc.gpsimd.affine_select(out=sel[:], in_=sel[:], compare_op=ALU.not_equal, fill=1.0, base=0,
                                    pattern=[[-1, E], [0, P]], channel_multiplier=1).then_inc(pool_set, 1)
            pool.wait_ge(pool_set, 5)
            nc.gpsimd.affine_select(out=sel[:], in_=sel[:], compare_op=ALU.not_equal, fill=1.0, base=-E,
                                    pattern=[[-1, E], [0, P]], channel_multiplier=1).then_inc(consts, 1)

            def setup_late():
                pool.wait_ge(prep_dve, 3)
                nc.gpsimd.tensor_tensor(sim_nrm[:], sim_sq[:], plus_half[:], ALU.pow).then_inc(nrm_root, 1)
                pool.wait_ge(wmax_done, 4)
                nc.gpsimd.partition_all_reduce(wmax_all[:], wmax[:], P, ABSMAX).then_inc(wmax_shared, 1)

            def body(i):
                g1, g2, gz = i + 2, i + 1, i
                if has(g1):
                    wait(pool, bn1_done, 2 * g1 + 2)
                    plain(pool)
                    nc.gpsimd.tensor_scalar(rstd1[:], mv1[:, :, 1], EPS, None, ALU.add).then_inc(rstd1_done, 1)
                    wait(pool, rstd1_done, 2 * g1 + 1)
                    nc.gpsimd.tensor_tensor(rstd1[:], rstd1[:], minus_half[:], ALU.pow).then_inc(rstd1_done, 1)
                if has(g2):
                    wait(pool, bn2_done, 2 * g2 + 2)
                    plain(pool)
                    nc.gpsimd.tensor_scalar(rstd2[:], mv2[:, :, 1], EPS, None, ALU.add)
                    wait(pool, rnorm_done, g2)
                    plain(pool)
                    nc.gpsimd.tensor_scalar(norm2[:], mv2[:, :, 1], float(C), None, ALU.mult).then_inc(rstd2_done, 1)
                    wait(pool, rstd2_done, 2 * g2 + 1)
                    nc.gpsimd.tensor_tensor(rstd2[:], rstd2[:], minus_half[:], ALU.pow)
                    nc.gpsimd.tensor_tensor(norm2[:], norm2[:], plus_half[:, 0:G], ALU.pow).then_inc(rstd2_done, 1)
                    wait(pool, rstd2_done, 2 * g2 + 2)
                    nc.gpsimd.tensor_tensor(norm2[:], norm2[:], rstd2[:], ALU.mult).then_inc(norm_step, 1)

                def z_low(g, e):
                    wait(pool, z_hi_done, E * g + e + 1)
                    nc.gpsimd.tensor_tensor(z[:, 1, e, :], z_full[:, e % Z_SLOTS, :], z[:, 0, e, :],
                                            ALU.subtract).then_inc(z_lo_done, 1)

                if has(gz):
                    for e in range(10, E):
                        z_low(gz, e)
                if has(i - 1):
                    g = i - 1
                    wait(pool, rsum_c_done, g + 1)
                    if isinstance(i, int):
                        pool.wait_ge(prep_dve, 6)
                    plain(pool)
                    nc.gpsimd.tensor_scalar(rs_c[:], rsum_c[:], out_scale[:], None, ALU.mult).then_inc(rs_c_done, 1)
                    wait(pool, rs_c_done, g + 1)
                    wait(pool, y_added, G * E * g)
                    plain(pool)
                    nc.gpsimd.tensor_tensor(w_out[:], w_all[:, bass.ds(G * g, G), :],
                                            rs_c[:].unsqueeze(2).broadcast_to([P, G, E]),
                                            ALU.mult).then_inc(w_out_done, 1)
                if isinstance(i, int) and i == -2:
                    setup_late()
                if has(g2):
                    for e in range(0, 10):
                        z_low(g2, e)

            passes(pool, body)

        @block.scalar
        def _(act):
            act.wait_ge(small_in, 16 * 7)
            nc.scalar.activation(tanh_x[:], gx[:], ACT.Tanh)
            nc.scalar.activation(tanh_f[:], gf[:], ACT.Tanh)
            nc.scalar.activation(sig[:], gates_b[:], ACT.Sigmoid).then_inc(tanh_done, 1)
            act.wait_ge(tanh_done, 1)
            act.wait_ge(prep_pe, 2)
            nc.scalar.activation(m_qk[:], acc_p[Q][:, 0:P], ACT.Copy)
            nc.scalar.activation(wvT[:], acc_p[K][:, 0:P], ACT.Copy, scale=tanh_x[:]).then_inc(tanh_done, 1)

            def weight_high():
                act.wait_ge(prep_dve, 5)
                for m in range(4):
                    nc.scalar.activation(w_hi[:, m], stage[:, m], ACT.Copy,
                                         scale=w_up[:, m:m + 1]).then_inc(hi_done, 1)

            def z_high(g, e):
                wait(act, z_full_done, E * g + e + 1)
                wait(act, expert_used, E * (g - 1) + e + 1)
                if isinstance(g, int) and g == 0:
                    act.wait_ge(lo_done, 4)
                nc.scalar.activation(z[:, 0, e, :], z_full[:, e % Z_SLOTS, :], ACT.Copy).then_inc(z_hi_done, 1)

            def body(i):
                g1, g2, gc = i + 2, i + 1, i - 1
                if isinstance(i, int) and i == -1:
                    weight_high()
                for s in range(E):
                    if s == 0 and has(gc):
                        wait(act, v_ps, gc + 1)
                        wait(act, oT_ps, gc)
                        nc.scalar.activation(v_sb[:].rearrange("p b h -> p (b h)"), m0[:],
                                             ACT.Copy).then_inc(v_tok_sb, 1)
                    if s == 2 and has(gc):
                        wait(act, cmax_done, 2 * gc + 2)
                        wait(act, cpT_ps, gc)
                        wait(act, rsum_c_done, gc)
                        for b in range(G):
                            last = nc.scalar.activation(pc[:, b, :], m1[:, tok(b)], ACT.Exp,
                                                        bias=nmax_c[:, b:b + 1], scale=score_scale[:],
                                                        accum_out=sum_c[:, b:b + 1])
                        last.then_inc(cexp_done, 1)
                    if s == 2 and has(g1):
                        wait(act, xnT_ps, g1 + 1)
                        wait(act, qxT_ps, g1)
                        nc.scalar.activation(xnT[:], m1[:], ACT.Copy).then_inc(xnT_sb, 1)
                    if s == 3 and has(g2):
                        wait(act, x2T_ps, g2 + 1)
                        wait(act, z_full_done, E * g2)
                        nc.scalar.activation(x2T[:], m0[:], ACT.Copy, scale=X_UP).then_inc(x2T_sb, 1)
                    if s == 5 and has(g2):
                        wait(act, gate_arg_done, g2 + 1)
                        nc.scalar.activation(gate_e[:], gate_arg[:], ACT.Exp).then_inc(gate_exp, 1)
                    if s == 5 and has(gc):
                        wait(act, cpT_ps, gc + 1)
                        wait(act, oT_ps, gc)
                        nc.scalar.activation(pcT[:], m1[:], ACT.Copy).then_inc(cpT_sb, 1)
                    if s == 6 and has(g1):
                        wait(act, qxT_ps, g1 + 1)
                        wait(act, xscore_ps, g1)
                        nc.scalar.activation(qxT[:], m0[:], ACT.Copy, scale=RSQRT_C).then_inc(qxT_sb, 1)
                        wait(act, ctxT_ps, g1 + 1)
                        wait(act, vx_ps, g1)
                        nc.scalar.activation(ctxT[:], m1[:, 0:G * S], ACT.Copy).then_inc(ctxT_sb, 1)
                    if s == 7 and has(g2):
                        wait(act, wT_ps, g2 + 1)
                        wait(act, wb_ps, E * g2)
                        nc.scalar.activation(w_splitT[:], m1[0:2 * E, 0:N // 2].bitcast(F16),
                                             ACT.Copy).then_inc(wT_sb, 1)
                    if s == 8 and has(gc):
                        wait(act, oT_ps, gc + 1)
                        wait(act, y_ps, 4 * G * gc)
                        nc.scalar.activation(o_hi[:], m0[:], ACT.Copy).then_inc(o_hi_done, 1)
                    if s == 9 and has(g1):
                        wait(act, xmax_done, g1 + 1)
                        wait(act, pxT_ps, g1)
                        wait(act, rsum_x_done, g1)
                        for b in range(G):
                            last = nc.scalar.activation(px[:, b, :], m1[:, b * S:(b + 1) * S], ACT.Exp,
                                                        bias=nmax_x[:, b:b + 1],
                                                        accum_out=sum_x[:, b:b + 1])
                        last.then_inc(xexp_done, 1)
                    if s == 10 and has(g1):
                        wait(act, vx_ps, g1 + 1)
                        wait(act, att_ps, g1)
                        nc.scalar.activation(vx[:], m0[0:S, :], ACT.Copy).then_inc(vx_sb, 1)
                    if s == 12 and has(g1):
                        wait(act, pxT_ps, g1 + 1)
                        nc.scalar.activation(pxT[:], m1[0:S, :], ACT.Copy).then_inc(pxT_sb, 1)
                    if s < 3 and has(i):
                        z_high(i, 10 + 2 * s)
                        z_high(i, 11 + 2 * s)
                    if s >= 8 and has(g2):
                        z_high(g2, s - 8)
                if has(i):
                    wait(act, cscore_ps, i)
                    wait(act, v_ps, i)
                    for m, dst in enumerate((qT, kT, vT)):
                        wait(act, acc_ps[m], i + 1)
                        nc.scalar.activation(dst[:], acc_p[m][:], ACT.Copy,
                                             scale=1.0 / (X_UP * W_UP)).then_inc(acc_sb[m], 1)
                if has(g2):
                    z_high(g2, 8)
                    z_high(g2, 9)

            passes(act, body)

        @block.vector
        def _(dve):
            def stats(g, src, bn, mv, done):
                plain(dve)
                for b in range(G):
                    last = nc.vector.bn_stats(bn[:, b, :], rows(src, g, b))
                last.then_inc(done, 1)
                wait(dve, done, 2 * g + 1)
                plain(dve)
                for b in range(G):
                    last = nc.vector.bn_aggr(mv[:, b, :], bn[:, b, :])
                last.then_inc(done, 1)

            def setup():
                dve.wait_ge(small_in, 16 * 7)
                nc.vector.tensor_tensor(sim_sq[:], sim_sb[:], sim_sb[:], ALU.mult).then_inc(prep_dve, 1)
                dve.wait_ge(consts, 1)
                nc.vector.tensor_copy(iota_f[:], iota_i[:]).then_inc(prep_dve, 1)
                dve.wait_ge(prep_pe, 3)
                nc.vector.tensor_copy(sim_sq[:], acc_p[V][:, 0:E]).then_inc(prep_dve, 1)

            def setup_weights():
                for m in range(4):
                    dve.wait_ge(proj_in[m], 16)
                    nc.vector.tensor_reduce(wmax[:, m:m + 1], stage[:, m].rearrange("p e h -> p (e h)"), AX_X,
                                            ALU.max, apply_absolute_value=True).then_inc(wmax_done, 1)
                dve.wait_ge(nrm_root, 1)
                step = prep_chain
                nc.vector.tensor_scalar(sim_nrm[:], sim_nrm[:], 1e-12, None, ALU.max).then_inc(step, 1)
                dve.wait_ge(step, 1)
                nc.vector.reciprocal(sim_nrm[:], sim_nrm[:]).then_inc(step, 1)
                dve.wait_ge(step, 2)
                nc.vector.tensor_tensor(sn[:], sim_sb[:], sim_nrm[:], ALU.mult).then_inc(prep_dve, 1)
                dve.wait_ge(wmax_shared, 1)
                nc.vector.tensor_scalar(wmax_all[:], wmax_all[:], 2.0 ** -60, 2.0 ** 60, ALU.max,
                                        ALU.min).then_inc(step, 1)
                dve.wait_ge(step, 3)
                nc.vector.tensor_scalar(w_pow[:].bitcast(U32), wmax_all[:].bitcast(U32), 0x7F800000, None,
                                        ALU.bitwise_and).then_inc(step, 1)
                dve.wait_ge(step, 4)
                nc.vector.reciprocal(w_up[:], w_pow[:]).then_inc(step, 1)
                nc.vector.tensor_scalar(score_scale[:], w_pow[:, Q:Q + 1], w_pow[:, K:K + 1], RSQRT_C,
                                        ALU.mult, ALU.mult)
                nc.vector.tensor_scalar(out_scale[:], w_pow[:, V:V + 1], w_pow[:, O:O + 1], 1.0 / W_UP,
                                        ALU.mult, ALU.mult).then_inc(step, 1)
                dve.wait_ge(step, 6)
                nc.vector.tensor_scalar(w_up[:], w_up[:], W_UP, None, ALU.mult).then_inc(prep_dve, 1)
                dve.wait_ge(tanh_done, 1)
                nc.vector.tensor_scalar(out_scale[:], out_scale[:], tanh_f[:], None, ALU.mult).then_inc(prep_dve, 1)

            def weight_low():
                for m in range(4):
                    dve.wait_ge(hi_done, m + 1)
                    nc.vector.scalar_tensor_tensor(
                        out=w_lo[:, m].rearrange("p e h -> p (e h)"), in0=stage[:, m].rearrange("p e h -> p (e h)"),
                        scalar=w_up[:, m:m + 1], in1=w_hi[:, m].rearrange("p e h -> p (e h)"),
                        op0=ALU.mult, op1=ALU.subtract).then_inc(lo_done, 1)

            def gate_first(g):
                def link(ins, n):
                    ins.then_inc(gate_step, 1)
                    dve.wait_ge(gate_step, GATE_STEPS * g + n)

                wait(dve, logit_ps, g + 1)
                lg = m0[:, 0:G * E].rearrange("p (b e) -> p b e", e=E)
                link(nc.vector.tensor_tensor(logit[:], lg, rnorm2[:].unsqueeze(2).broadcast_to([P, G, E]),
                                             ALU.mult), 1)
                link(nc.vector.tensor_tensor(logit[:], logit[:], sig[:].unsqueeze(1).broadcast_to([P, G, E]),
                                             ALU.subtract), 2)
                plain(dve)
                for b in range(G):
                    last = nc.vector.max(top[:, b, :], logit[:, b, :])
                link(last, 3)
                plain(dve)
                for b in range(G):
                    nc.vector.max_index(top_at[:, b, :], top[:, b, :], logit[:, b, :])
                nc.vector.tensor_scalar(inactive[:], top[:, :, 0], 0.0, None, ALU.is_le)
                link(nc.vector.tensor_scalar(gate_max[:], top[:, :, 0], 0.0, None, ALU.max), 4)
                nc.vector.scalar_tensor_tensor(out=gate_arg[:], in0=logit[:], scalar=0.0,
                                               in1=gate_max[:].unsqueeze(2).broadcast_to([P, G, E]),
                                               op0=ALU.max, op1=ALU.subtract).then_inc(gate_arg_done, 1)
                iota_b = iota_f[:].unsqueeze(1).broadcast_to([P, G, E])
                nc.vector.tensor_tensor(fb0[:], iota_b, top_at[:, :, 0:1].broadcast_to([P, G, E]), ALU.is_equal)
                link(nc.vector.tensor_tensor(fb1[:], iota_b, top_at[:, :, 1:2].broadcast_to([P, G, E]),
                                             ALU.is_equal), 5)
                link(nc.vector.tensor_tensor(fb0[:], fb0[:], fb1[:], ALU.add), 6)
                link(nc.vector.tensor_tensor(fb0[:], fb0[:], inactive[:].unsqueeze(2).broadcast_to([P, G, E]),
                                             ALU.mult), 7)
                link(nc.vector.scalar_tensor_tensor(out=mask[:], in0=logit[:], scalar=0.0, in1=fb0[:],
                                                    op0=ALU.is_gt, op1=ALU.add), EXP_AT)

            def gate_second(g):
                def link(ins, n):
                    ins.then_inc(gate_step, 1)
                    dve.wait_ge(gate_step, GATE_STEPS * g + n)

                w_g = w_all[:, bass.ds(G * g, G), :]
                wait(dve, gate_exp, g + 1)
                link(nc.vector.tensor_tensor(mask[:], gate_e[:], mask[:], ALU.mult), EXP_AT + 1)
                link(nc.vector.reduce_sum(wsum[:], mask[:], AX_X), EXP_AT + 2)
                link(nc.vector.reciprocal(wsum[:], wsum[:]), EXP_AT + 3)
                link(nc.vector.tensor_tensor(w_g, mask[:], wsum[:].unsqueeze(2).broadcast_to([P, G, E]),
                                             ALU.mult), EXP_AT + 4)
                wait(dve, wT_ps, g)
                plain(dve)
                link(nc.vector.tensor_copy(w_split[:, :, 0:E], w_g), EXP_AT + 5)
                nc.vector.tensor_tensor(w_split[:, :, E:2 * E], w_g, w_split[:, :, 0:E],
                                        ALU.subtract).then_inc(w_ready, 1)

            def z_scale(g, e):
                n = E * g + e
                wait(dve, wb_ps, n + 1)
                wait(dve, z_lo_done, n - Z_SLOTS + 1)
                nc.vector.tensor_tensor(z_full[:, e % Z_SLOTS, :], wb_p[e % 2][:], x2T[:],
                                        ALU.mult).then_inc(z_full_done, 1)

            def add_experts(g, k):
                b, q = divmod(k, E // 4)
                wait(dve, y_ps, 4 * G * g + k + 1)
                if k == 0:
                    wait(dve, w_out_done, g + 1)
                for j in range(4):
                    e = 4 * q + j
                    if e > 0:
                        wait(dve, y_added, G * E * g + E * b + e)
                    nc.vector.scalar_tensor_tensor(
                        out=rows(x_all, g, b), in0=y_p[:, tok(j)], scalar=w_out[:, b, e:e + 1],
                        in1=rows(x_all, g, b), op0=ALU.mult, op1=ALU.add).then_inc(y_added, 1)

            def normed(g, dst, mv, rstd, done):
                for b in range(G):
                    last = nc.vector.tensor_scalar(dst[:, b, :], rows(x_all, g, b), mv[:, b, 0:1],
                                                   rstd[:, b:b + 1], ALU.subtract, ALU.mult)
                last.then_inc(done, 1)

            def first_stats(g):
                if isinstance(g, int):
                    dve.wait_ge(x_in[g * G // CHUNK], 16)
                stats(g, x_all, bn1, mv1, bn1_done)

            def body(i):
                g1, g2, gc, gd = i + 2, i + 1, i - 1, i - 2
                if has(g1):
                    first_stats(g1)
                if isinstance(i, int) and i == -2:
                    setup()
                if has(g2):
                    wait(dve, x1_done, g2 + 1)
                    stats(g2, x_all, bn2, mv2, bn2_done)
                if isinstance(i, int) and i == -1:
                    setup_weights()
                for s in range(E):
                    if s == 1 and has(gc):
                        wait(dve, cscore_ps, gc + 1)
                        wait(dve, cexp_done, gc)
                        nc.vector.tensor_reduce(nmax_c[:], m1[:].rearrange("p (b t) -> p b t", b=G), AX_X,
                                                ALU.max, negate=True).then_inc(cmax_done, 1)
                        wait(dve, cmax_done, 2 * gc + 1)
                        nc.vector.tensor_scalar(nmax_c[:], nmax_c[:], score_scale[:], None,
                                                ALU.mult).then_inc(cmax_done, 1)
                    if s == 1 and has(g1):
                        wait(dve, rstd1_done, 2 * g1 + 2)
                        wait(dve, xnT_ps, g1)
                        normed(g1, xn, mv1, rstd1, xn_done)
                    if s == 2 and has(g2):
                        wait(dve, rstd2_done, 2 * g2 + 2)
                        wait(dve, x2T_ps, g2)
                        normed(g2, x2, mv2, rstd2, x2_done)
                    if s == 3 and has(g2):
                        wait(dve, norm_step, g2 + 1)
                        nc.vector.tensor_scalar(rnorm2[:], norm2[:], 1e-12, X_UP, ALU.max,
                                                ALU.mult).then_inc(rnorm_done, 1)
                        wait(dve, rnorm_done, g2 + 1)
                        nc.vector.reciprocal(rnorm2[:], rnorm2[:]).then_inc(rnorm_inv, 1)
                    if s == 4 and has(g2):
                        wait(dve, rnorm_inv, g2 + 1)
                        gate_first(g2)
                    if s == 5 and has(g2):
                        gate_second(g2)
                    if s == 5 and has(gc):
                        wait(dve, cexp_done, gc + 1)
                        wait(dve, rs_c_done, gc)
                        nc.vector.reciprocal(rsum_c[:], sum_c[:]).then_inc(rsum_c_done, 1)
                    if s == 8 and has(gc):
                        wait(dve, o_hi_done, gc + 1)
                        nc.vector.tensor_tensor(o_lo[:], m0[:], o_hi[:], ALU.subtract).then_inc(o_lo_done, 1)
                    if s == 9 and has(g1):
                        wait(dve, xscore_ps, g1 + 1)
                        wait(dve, xexp_done, g1)
                        nc.vector.tensor_reduce(nmax_x[:], m1[:, 0:G * S].rearrange("p (b t) -> p b t", b=G),
                                                AX_X, ALU.max, negate=True).then_inc(xmax_done, 1)
                    if s == 12 and has(g1):
                        wait(dve, xexp_done, g1 + 1)
                        nc.vector.reciprocal(rsum_x[:], sum_x[:]).then_inc(rsum_x_done, 1)
                    if s == 14 and has(g1):
                        wait(dve, att_ps, g1 + 1)
                        wait(dve, rsum_x_done, g1 + 1)
                        for b in range(G):
                            last = nc.vector.scalar_tensor_tensor(
                                out=rows(x_all, g1, b), in0=m0[:, tok(b)], scalar=rsum_x[:, b:b + 1],
                                in1=rows(x_all, g1, b), op0=ALU.mult, op1=ALU.add)
                        last.then_inc(x1_done, 1)
                    if s == 8 and isinstance(i, int) and i == -1:
                        weight_low()
                    if s < 3 and has(i):
                        z_scale(i, 10 + 2 * s)
                        z_scale(i, 11 + 2 * s)
                    if s >= 8 and has(g2):
                        z_scale(g2, s - 8)
                    if s < 8 and has(gd):
                        add_experts(gd, 8 + s)
                    if s >= 9 and has(gc):
                        add_experts(gc, s - 9)
                if has(g2):
                    z_scale(g2, 8)
                if has(gc):
                    add_experts(gc, 7)
                if has(g2):
                    z_scale(g2, 9)

            passes(dve, body, x_in)

        @block.tensor
        def _(pe):
            pe.wait_ge(small_in, 16 * 7)
            pe.wait_ge(consts, 1)
            nc.tensor.matmul(acc_p[Q][:, 0:P], wq_sb[:], wk_sb[:], start=True, stop=True).then_inc(prep_pe, 1)
            nc.tensor.transpose(acc_p[K][:, 0:P], wv_sb[:], ident[:]).then_inc(prep_pe, 1)
            pe.wait_ge(prep_dve, 1)
            nc.tensor.matmul(acc_p[V][:, 0:E], ones[:], sim_sq[:], start=True, stop=True).then_inc(prep_pe, 1)

            def broadcast_weights(g, e):
                n = E * g + e
                if e == 0:
                    wait(pe, wT_sb, g + 1)
                wait(pe, z_full_done, n - 1)
                nc.tensor.matmul(wb_p[e % 2][:], sel[:, e, :], w_splitT[:], start=True, stop=True).then_inc(wb_ps, 1)

            def out_chunk(g, k):
                b, q = divmod(k, E // 4)
                if k == 0:
                    wait(pe, o_lo_done, g + 1)
                wait(pe, y_added, G * E * g + 4 * k)
                for n, (lhs, rhs) in enumerate(((o_hi, w_hi), (o_hi, w_lo), (o_lo, w_hi))):
                    last = nc.tensor.matmul(y_p[:], lhs[:, tok(b)],
                                            rhs[:, O, 4 * q:4 * q + 4, :].rearrange("p e h -> p (e h)"),
                                            start=(n == 0), stop=(n == 2))
                last.then_inc(y_ps, 1)

            def body(i):
                g1, g2, gc, gd = i + 2, i + 1, i - 1, i - 2
                for s in range(E):
                    if has(i):
                        wait(pe, z_lo_done, E * i + s + 1)
                        for m in (Q, K, V):
                            if s == 0:
                                wait(pe, acc_sb[m], i)
                            for n, (w, half) in enumerate(((w_hi, 0), (w_lo, 0), (w_hi, 1))):
                                last = nc.tensor.matmul(acc_p[m][:], w[:, m, s, :], z[:, half, s, :],
                                                        start=(s == 0 and n == 0), stop=(s == E - 1 and n == 2))
                            if s == E - 1:
                                last.then_inc(acc_ps[m], 1)
                        if s < E - 1:
                            last.then_inc(expert_used, 1)
                        else:
                            pe.sem_inc(expert_used, 1)
                    if s < 8 and has(gd):
                        out_chunk(gd, 8 + s)
                    if s >= 9 and has(gc):
                        out_chunk(gc, s - 9)
                    if s == 0 and has(gc):
                        wait(pe, acc_sb[V], gc + 1)
                        wait(pe, x1_done, cap(i + 2))
                        if isinstance(i, int):
                            wait(pe, o_lo_done, gc)
                        for b in range(G):
                            last = nc.tensor.transpose(m0[:, tok(b)], vT[:, tok(b)], ident[:])
                        last.then_inc(v_ps, 1)
                    if s == 1 and has(gc):
                        wait(pe, acc_sb[K], gc + 1)
                        wait(pe, pxT_sb, cap(i + 2))
                        for b in range(G):
                            last = nc.tensor.matmul(m1[:, tok(b)], qT[:, tok(b)], kT[:, tok(b)],
                                                    start=True, stop=True)
                        last.then_inc(cscore_ps, 1)
                    if s == 2 and has(g1):
                        wait(pe, xn_done, g1 + 1)
                        wait(pe, cexp_done, cap(i))
                        for b in range(G):
                            last = nc.tensor.transpose(m1[:, tok(b)], xn[:, b, :], ident[:])
                        last.then_inc(xnT_ps, 1)
                    if s == 3 and has(g2):
                        wait(pe, x2_done, g2 + 1)
                        wait(pe, v_tok_sb, cap(i))
                        for b in range(G):
                            last = nc.tensor.transpose(m0[:, tok(b)], x2[:, b, :], ident[:])
                        last.then_inc(x2T_ps, 1)
                    if s == 4 and has(g2):
                        if isinstance(i, int) and i == -1:
                            pe.wait_ge(prep_dve, 4)
                        wait(pe, x2T_sb, g2 + 1)
                        for b in range(G):
                            last = nc.tensor.matmul(m0[:, b * E:(b + 1) * E], x2T[:, tok(b)], sn[:],
                                                    start=True, stop=True)
                        last.then_inc(logit_ps, 1)
                    if s == 5 and has(gc):
                        wait(pe, cexp_done, gc + 1)
                        wait(pe, xnT_sb, cap(i + 3))
                        for b in range(G):
                            last = nc.tensor.transpose(m1[:, tok(b)], pc[:, b, :], ident[:])
                        last.then_inc(cpT_ps, 1)
                    if s == 6 and has(g1):
                        if isinstance(i, int) and i == -2:
                            pe.wait_ge(tanh_done, 2)
                        wait(pe, xnT_sb, g1 + 1)
                        if not (isinstance(i, int) and i == -2):
                            wait(pe, gate_step, GATE_STEPS * (i + 1) + 1)
                        nc.tensor.matmul(m0[:], m_qk[:], xnT[:], start=True, stop=True).then_inc(qxT_ps, 1)
                        wait(pe, ctx_loaded, 16 * g1 + 16)
                        wait(pe, cpT_sb, cap(i))
                        for b in range(G):
                            last = nc.tensor.transpose(m1[:, b * S:(b + 1) * S], ctx_g[:, b, :],
                                                       ident[0:S, 0:S])
                        last.then_inc(ctxT_ps, 1)
                    if s == 7 and has(g2):
                        wait(pe, w_ready, g2 + 1)
                        wait(pe, ctxT_sb, cap(i + 3))
                        if isinstance(i, int):
                            wait(pe, cpT_sb, cap(i))
                        for b in range(G):
                            last = nc.tensor.transpose(m1[0:2 * E, b * P // 2:(b + 1) * P // 2].bitcast(F16),
                                                       w_split[:, b, :], ident16[:])
                        last.then_inc(wT_ps, 1)
                    if s == 8 and has(gc):
                        wait(pe, v_tok_sb, gc + 1)
                        wait(pe, cpT_sb, gc + 1)
                        wait(pe, qxT_sb, cap(i + 3))
                        if isinstance(i, int):
                            wait(pe, gate_step, GATE_STEPS * (cap(i + 2) - 1) + 1)
                        for b in range(G):
                            last = nc.tensor.matmul(m0[:, tok(b)], v_sb[:, b, :], pcT[:, tok(b)],
                                                    start=True, stop=True)
                        last.then_inc(oT_ps, 1)
                    if s == 9 and has(g1):
                        wait(pe, qxT_sb, g1 + 1)
                        wait(pe, ctxT_sb, g1 + 1)
                        wait(pe, wT_sb, cap(i + 2))
                        for b in range(G):
                            last = nc.tensor.matmul(m1[:, b * S:(b + 1) * S], qxT[:, tok(b)],
                                                    ctxT[:, b * S:(b + 1) * S], start=True, stop=True)
                        last.then_inc(xscore_ps, 1)
                    if s == 10 and has(g1):
                        wait(pe, o_lo_done, cap(i))
                        for b in range(G):
                            last = nc.tensor.matmul(m0[0:S, tok(b)], ctxT[:, b * S:(b + 1) * S], wvT[:],
                                                    start=True, stop=True)
                        last.then_inc(vx_ps, 1)
                    if s == 12 and has(g1):
                        wait(pe, xexp_done, g1 + 1)
                        for b in range(G):
                            last = nc.tensor.transpose(m1[0:S, tok(b)], px[:, b, :], ident[:])
                        last.then_inc(pxT_ps, 1)
                    if s == 14 and has(g1):
                        wait(pe, pxT_sb, g1 + 1)
                        wait(pe, vx_sb, g1 + 1)
                        for b in range(G):
                            last = nc.tensor.matmul(m0[:, tok(b)], pxT[:, tok(b)], vx[:, tok(b)],
                                                    start=True, stop=True)
                        last.then_inc(att_ps, 1)
                    if s < 3 and has(i):
                        broadcast_weights(i, 10 + 2 * s)
                        broadcast_weights(i, 11 + 2 * s)
                    if s >= 8 and has(g2):
                        broadcast_weights(g2, s - 8)
                if has(g2):
                    broadcast_weights(g2, 8)
                if has(gc):
                    out_chunk(gc, 7)
                if has(g2):
                    broadcast_weights(g2, 9)

            passes(pe, body)


_INS = ['x', 'ctx_1024', 'g_xattn', 'g_ffn', 'L0_xattn_Wk', 'L0_xattn_Wq', 'L0_xattn_Wv', 'L0_ffn_sim_matrix',
        'L0_ffn_gates', 'L0_ffn_q_proj', 'L0_ffn_k_proj', 'L0_ffn_v_proj', 'L0_ffn_o_proj']


def kernel(**inputs):
    import numpy as _np
    import concourse.bacc as _bacc
    from concourse import mybir as _mybir
    from concourse.bass_utils import run_bass_kernel_spmd as _run

    nc = _bacc.Bacc("TRN2", target_bir_lowering=False, num_devices=1)
    arrays, args = {}, []
    for name in _INS:
        a = _np.ascontiguousarray(inputs[name])
        arrays[f"in_{name}_dram"] = a
        args.append(nc.dram_tensor(f"in_{name}_dram", a.shape, _mybir.dt.from_np(a.dtype), kind="ExternalInput").ap())
    out = nc.dram_tensor("out_dram", arrays["in_x_dram"].shape, _mybir.dt.float32, kind="ExternalOutput").ap()
    flamingo_gated_moe_attention(nc, *args, out)
    r = _run(nc, [arrays], core_ids=[0])
    return r.results[0]["out_dram"]
```

```python
from contextlib import ExitStack

import concourse.bass as bass
from concourse import mybir

ALU = mybir.AluOpType
ACT = mybir.ActivationFunctionType
F32 = mybir.dt.float32
F16 = mybir.dt.float16
U32 = mybir.dt.uint32
I32 = mybir.dt.int32
AX_X = mybir.AxisListType.X
ABSMAX = bass.bass_isa.ReduceOp.absmax

P = 128
G = 4
Q, K, V, O = range(4)
EPS = 1e-5
X_UP = 4096.0
W_UP = 16384.0
Z_SLOTS = 4
SUM_SLOTS = 8
SUM_STEPS = 6
GATE_STEPS = 13
EXP_AT = 8


Z_LATE = {0: (10, 11), 1: (12, 13), 2: (14, 15)}
Z_EARLY = {8: (0,), 9: (1,), 10: (2, 3), 11: (4,), 12: (5, 6), 13: (7,), 14: (8,), 15: (9,)}

EARLY = 10


def flamingo_gated_moe_attention(nc, x, ctx_in, g_xattn, g_ffn, Wk, Wq, Wv, sim_matrix, gates,
                                 q_proj, k_proj, v_proj, o_proj, out):
    B, T, C = x.shape
    _, S, _ = ctx_in.shape
    E = sim_matrix.shape[1]
    assert T == P and C == P and E == 16 and B % G == 0
    NG = B // G
    N = G * P
    LOOP = (3, NG - 3)
    CHUNK = B // 4
    RSQRT_C = float(P) ** -0.5

    with ExitStack() as ctx:
        def sb(name, shape, dt=F32):
            return ctx.enter_context(nc.sbuf_tensor(name, shape, dt))

        def psum(name):
            return ctx.enter_context(nc.psum_tensor(name, [P, N], F32))

        def sem(name):
            return ctx.enter_context(nc.semaphore(name))

        x_all = sb("x_all", [P, B, C])
        ctx_g = sb("ctx_g", [S, G, C])
        w_hi = sb("w_hi", [P, 4, E, P], F16)
        w_lo = sb("w_lo", [P, 4, E, P], F16)
        w_all = sb("w_all", [P, B, E])
        z = sb("z", [P, 2, E, N], F16)
        stage = sb("stage", [P, 4, E, P])
        z_full = sb("z_full", [P, Z_SLOTS, N])
        ident = sb("ident", [P, P])
        ident16 = sb("ident16", [P, P], F16)
        ones = sb("ones", [P, P])
        sel = sb("sel", [2 * E, E, P], F16)
        iota_i = sb("iota_i", [P, E], I32)
        iota_f = sb("iota_f", [P, E])
        minus_half = sb("minus_half", [P, G])
        plus_half = sb("plus_half", [P, E])
        gx = sb("gx", [P, 1])
        gf = sb("gf", [P, 1])
        tanh_x = sb("tanh_x", [P, 1])
        tanh_f = sb("tanh_f", [P, 1])
        gates_b = sb("gates_b", [P, E])
        sig = sb("sig", [P, E])
        sim_sb = sb("sim_sb", [P, E])
        sim_sq = sb("sim_sq", [P, E])
        sim_nrm = sb("sim_nrm", [P, E])
        sn = sb("sn", [P, E])
        wk_sb = sb("wk_sb", [P, P])
        wq_sb = sb("wq_sb", [P, P])
        wv_sb = sb("wv_sb", [P, P])
        m_qk = sb("m_qk", [P, P])
        wvT = sb("wvT", [P, P])
        wmax = sb("wmax", [P, 4])
        wmax_all = sb("wmax_all", [P, 4])
        w_pow = sb("w_pow", [P, 4])
        w_up = sb("w_up", [P, 4])
        score_scale = sb("score_scale", [P, 1])
        out_scale = sb("out_scale", [P, 1])
        bn1 = sb("bn1", [P, G, 6])
        mv1 = sb("mv1", [P, G, 2])
        rstd1 = sb("rstd1", [P, G])
        xn = sb("xn", [P, G, C])
        xnT = sb("xnT", [P, N])
        qxT = sb("qxT", [P, N])
        ctxT = sb("ctxT", [P, G * S])
        nmax_x = sb("nmax_x", [P, G])
        px = sb("px", [P, G, S])
        sum_x = sb("sum_x", [P, G])
        rsum_x = sb("rsum_x", [P, G])
        pxT = sb("pxT", [S, N])
        vx = sb("vx", [S, N])
        bn2 = sb("bn2", [P, G, 6])
        mv2 = sb("mv2", [P, G, 2])
        rstd2 = sb("rstd2", [P, G])
        norm2 = sb("norm2", [P, G])
        rnorm2 = sb("rnorm2", [P, G])
        x2 = sb("x2", [P, G, C])
        x2T = sb("x2T", [P, N])
        logit = sb("logit", [P, G, E])
        top = sb("top", [P, G, 8])
        top_at = sb("top_at", [P, G, 8], U32)
        gate_max = sb("gate_max", [P, G])
        inactive = sb("inactive", [P, G])
        gate_arg = sb("gate_arg", [P, G, E])
        gate_e = sb("gate_e", [P, G, E])
        fb0 = sb("fb0", [P, G, E])
        fb1 = sb("fb1", [P, G, E])
        mask = sb("mask", [P, G, E])
        wsum = sb("wsum", [P, G])
        w_split = sb("w_split", [P, G, 2 * E], F16)
        w_splitT = sb("w_splitT", [2 * E, N], F16)
        qT = sb("qT", [P, N])
        kT = sb("kT", [P, N])
        vT = sb("vT", [P, N])
        v_sb = sb("v_sb", [P, G, P])
        nmax_c = sb("nmax_c", [P, G])
        pc = sb("pc", [P, G, P])
        sum_c = sb("sum_c", [P, G])
        rsum_c = sb("rsum_c", [P, G])
        rs_c = sb("rs_c", [P, G])
        pcT = sb("pcT", [P, N])
        o_hi = sb("o_hi", [P, N], F16)
        o_lo = sb("o_lo", [P, N], F16)
        w_out = sb("w_out", [P, G, E])
        parts = sb("parts", [P, SUM_SLOTS, 4, P])
        acc_p = [psum("acc_q"), psum("acc_k"), psum("acc_v")]
        wb_p = psum("wb")
        y_p = [psum("y0"), psum("y1")]
        m0 = psum("m0")
        m1 = psum("m1")

        x_in = [sem(f"x_in{c}") for c in range(4)]
        ctx_loaded = sem("ctx_loaded")
        small_in = sem("small_in")
        proj_in = [sem(f"proj_in{m}") for m in range(4)]
        out_stored = sem("out_stored")
        pool_set = sem("pool_set")
        consts = sem("consts")
        passed = sem("passed")
        tanh_done = sem("tanh_done")
        prep_pe = sem("prep_pe")
        prep_dve = sem("prep_dve")
        prep_chain = sem("prep_chain")
        wmax_done = sem("wmax_done")
        wmax_shared = sem("wmax_shared")
        hi_done = sem("hi_done")
        lo_done = sem("lo_done")
        nrm_root = sem("nrm_root")
        bn1_done = sem("bn1_done")
        rstd1_done = sem("rstd1_done")
        xn_done = sem("xn_done")
        xnT_ps = sem("xnT_ps")
        xnT_sb = sem("xnT_sb")
        qxT_ps = sem("qxT_ps")
        qxT_sb = sem("qxT_sb")
        ctxT_ps = sem("ctxT_ps")
        ctxT_sb = sem("ctxT_sb")
        xscore_ps = sem("xscore_ps")
        xmax_done = sem("xmax_done")
        xexp_done = sem("xexp_done")
        vx_ps = sem("vx_ps")
        vx_sb = sem("vx_sb")
        pxT_ps = sem("pxT_ps")
        pxT_sb = sem("pxT_sb")
        att_ps = sem("att_ps")
        rsum_x_done = sem("rsum_x_done")
        x1_done = sem("x1_done")
        bn2_done = sem("bn2_done")
        rstd2_done = sem("rstd2_done")
        norm_step = sem("norm_step")
        rnorm_done = sem("rnorm_done")
        rnorm_inv = sem("rnorm_inv")
        x2_done = sem("x2_done")
        x2T_ps = sem("x2T_ps")
        x2T_sb = sem("x2T_sb")
        logit_ps = sem("logit_ps")
        gate_step = sem("gate_step")
        gate_arg_done = sem("gate_arg_done")
        gate_exp = sem("gate_exp")
        w_ready = sem("w_ready")
        wT_ps = sem("wT_ps")
        wT_sb = sem("wT_sb")
        wb_ps = sem("wb_ps")
        z_full_done = sem("z_full_done")
        z_hi_done = sem("z_hi_done")
        lo_pool = sem("lo_pool")
        lo_dve = sem("lo_dve")
        expert_used = sem("expert_used")
        acc_ps = [sem("q_ps"), sem("k_ps"), sem("v_ps")]
        acc_sb = [sem("q_sb"), sem("k_sb"), sem("vT_sb")]
        v_ps = sem("v_tok_ps")
        v_tok_sb = sem("v_tok_sb")
        cscore_ps = sem("cscore_ps")
        cmax_done = sem("cmax_done")
        cexp_done = sem("cexp_done")
        cpT_ps = sem("cpT_ps")
        cpT_sb = sem("cpT_sb")
        oT_ps = sem("oT_ps")
        o_hi_done = sem("o_hi_done")
        o_lo_done = sem("o_lo_done")
        rsum_c_done = sem("rsum_c_done")
        rs_c_done = sem("rs_c_done")
        w_out_done = sem("w_out_done")
        y_ps = sem("y_ps")
        y_scaled = sem("y_scaled")
        sum_step = sem("sum_step")

        block = ctx.enter_context(nc.Block())

        def wait(eng, s, count):
            if not isinstance(count, int) or count > 0:
                eng.wait_ge(s, count)

        def plain(eng):
            eng.sem_inc(passed, 1)

        def cap(groups):
            return min(groups, NG) if isinstance(groups, int) else groups

        def has(g):
            return not isinstance(g, int) or 0 <= g < NG

        def passes(eng, body, loads=()):
            for i in range(-2, LOOP[0]):
                body(i)
            for load in loads:
                eng.wait_ge(load, 16)
            with eng.Fori(LOOP[0], LOOP[1]) as i:
                body(i)
            for i in range(LOOP[1], NG + 2):
                body(i)

        def z_work(i, s):
            late = [(i, e) for e in Z_LATE.get(s, ())] if has(i) else []
            return late + ([(i + 1, e) for e in Z_EARLY.get(s, ())] if has(i + 1) else [])

        def wait_low(eng, g, e):
            if e < EARLY:
                wait(eng, lo_pool, EARLY * g + e + 1)
            else:
                wait(eng, lo_dve, (E - EARLY) * g + e - EARLY + 1)

        def rows(t, g, b):
            return t[:, bass.ds(G * g + b, 1), :].rearrange("p a c -> p (a c)")

        def tok(b):
            return slice(b * P, (b + 1) * P)

        @block.sync
        def _(sp):
            x_v = x.rearrange("b n c -> n b c")
            c_v = ctx_in.rearrange("b s c -> s b c")
            sp.dma_start(x_all[:, 0:CHUNK, :], x_v[:, 0:CHUNK, :]).then_inc(x_in[0], 16)
            for dst, src in ((wq_sb, Wq), (wk_sb, Wk), (wv_sb, Wv), (sim_sb, sim_matrix)):
                sp.dma_start(dst[:], src).then_inc(small_in, 16)
            sp.dma_start(gx[:], g_xattn.partition_broadcast(P)).then_inc(small_in, 16)
            sp.dma_start(gf[:], g_ffn.partition_broadcast(P)).then_inc(small_in, 16)
            sp.dma_start(gates_b[:], gates.partition_broadcast(P)).then_inc(small_in, 16)
            sp.dma_start(ctx_g[:], c_v[:, 0:G, :]).then_inc(ctx_loaded, 16)
            for m, w in enumerate((q_proj, k_proj, v_proj, o_proj)):
                sp.dma_start(stage[:, m], w.rearrange("e c h -> c e h")).then_inc(proj_in[m], 16)
            for c in range(1, 4):
                sp.dma_start(x_all[:, c * CHUNK:(c + 1) * CHUNK, :],
                             x_v[:, c * CHUNK:(c + 1) * CHUNK, :]).then_inc(x_in[c], 16)
            o_v = out.rearrange("b n c -> n b c")

            def load_context(g):
                sp.wait_ge(ctxT_ps, g)
                sp.dma_start(ctx_g[:], c_v[:, bass.ds(G * g, G), :]).then_inc(ctx_loaded, 16)

            def store(g):
                sp.wait_ge(sum_step, G * SUM_STEPS * g + G * SUM_STEPS)
                sp.dma_start(o_v[:, bass.ds(G * g, G), :], x_all[:, bass.ds(G * g, G), :]).then_inc(out_stored, 16)

            for g in range(1, 5):
                load_context(g)
            with sp.Fori(5, NG) as g:
                load_context(g)
                store(g - 5)
            for g in range(NG - 5, NG):
                store(g)
            sp.wait_ge(out_stored, 16 * NG)

        @block.gpsimd
        def _(pool):
            nc.gpsimd.memset(ident[:], 0.0).then_inc(pool_set, 1)
            nc.gpsimd.memset(ident16[:], 0.0).then_inc(pool_set, 1)
            nc.gpsimd.memset(sel[:], 0.0).then_inc(pool_set, 1)
            nc.gpsimd.memset(ones[:], 1.0)
            nc.gpsimd.memset(minus_half[:], -0.5)
            nc.gpsimd.memset(plus_half[:], 0.5)
            nc.gpsimd.iota(iota_i[:], pattern=[[1, E]], base=0, channel_multiplier=0).then_inc(pool_set, 1)
            pool.wait_ge(pool_set, 4)
            for m in (ident, ident16):
                nc.gpsimd.affine_select(out=m[:], in_=m[:], compare_op=ALU.not_equal, fill=1.0, base=0,
                                        pattern=[[-1, P]], channel_multiplier=1)
            nc.gpsimd.affine_select(out=sel[:], in_=sel[:], compare_op=ALU.not_equal, fill=1.0, base=0,
                                    pattern=[[-1, E], [0, P]], channel_multiplier=1).then_inc(pool_set, 1)
            pool.wait_ge(pool_set, 5)
            nc.gpsimd.affine_select(out=sel[:], in_=sel[:], compare_op=ALU.not_equal, fill=1.0, base=-E,
                                    pattern=[[-1, E], [0, P]], channel_multiplier=1).then_inc(consts, 1)

            def setup_norms():
                pool.wait_ge(prep_dve, 3)
                nc.gpsimd.tensor_tensor(sim_nrm[:], sim_sq[:], plus_half[:], ALU.pow).then_inc(nrm_root, 1)

            def setup_max():
                pool.wait_ge(wmax_done, 4)
                nc.gpsimd.partition_all_reduce(wmax_all[:], wmax[:], P, ABSMAX).then_inc(wmax_shared, 1)

            def first_rstd(g):
                wait(pool, bn1_done, 2 * g + 2)
                plain(pool)
                nc.gpsimd.tensor_scalar(rstd1[:], mv1[:, :, 1], EPS, None, ALU.add).then_inc(rstd1_done, 1)
                wait(pool, rstd1_done, 2 * g + 1)
                nc.gpsimd.tensor_tensor(rstd1[:], rstd1[:], minus_half[:], ALU.pow).then_inc(rstd1_done, 1)

            def second_rstd(g):
                wait(pool, bn2_done, 2 * g + 2)
                plain(pool)
                nc.gpsimd.tensor_scalar(rstd2[:], mv2[:, :, 1], EPS, None, ALU.add)
                wait(pool, rnorm_done, g)
                plain(pool)
                nc.gpsimd.tensor_scalar(norm2[:], mv2[:, :, 1], float(C), None, ALU.mult).then_inc(rstd2_done, 1)
                wait(pool, rstd2_done, 2 * g + 1)
                nc.gpsimd.tensor_tensor(rstd2[:], rstd2[:], minus_half[:], ALU.pow).then_inc(rstd2_done, 1)
                nc.gpsimd.tensor_tensor(norm2[:], norm2[:], plus_half[:, 0:G], ALU.pow).then_inc(norm_step, 1)
                wait(pool, norm_step, 2 * g + 1)
                nc.gpsimd.tensor_tensor(norm2[:], norm2[:], rstd2[:], ALU.mult).then_inc(norm_step, 1)

            def body(i):
                g1, g2, gc, gd = i + 2, i + 1, i - 1, i - 2
                if isinstance(i, int) and i == -2:
                    first_rstd(0)

                def z_low(g, e):
                    wait(pool, z_hi_done, E * g + e + 1)
                    nc.gpsimd.tensor_tensor(z[:, 1, e, :], z_full[:, e % Z_SLOTS, :], z[:, 0, e, :],
                                            ALU.subtract).then_inc(lo_pool, 1)

                def sum_pairs(g, k):
                    b, q = divmod(k, E // 4)
                    slot = k % SUM_SLOTS
                    if k in (4, 8, 12):
                        sum_rest(g, b - 1)
                    if q % 2 == 1:
                        wait(pool, y_scaled, 4 * G * g + k + 1)
                        nc.gpsimd.tensor_tensor(parts[:, slot - 1], parts[:, slot - 1], parts[:, slot],
                                                ALU.add).then_inc(sum_step, 1)
                    if k == 4 * G - 1:
                        sum_rest(g, G - 1)

                def sum_rest(g, b):
                    first = 4 * b % SUM_SLOTS
                    n = SUM_STEPS * (G * g + b)
                    wait(pool, sum_step, n + 2)
                    nc.gpsimd.tensor_tensor(parts[:, first], parts[:, first], parts[:, first + 2],
                                            ALU.add).then_inc(sum_step, 1)
                    wait(pool, sum_step, n + 3)
                    nc.gpsimd.tensor_tensor(parts[:, first, 0:2], parts[:, first, 0:2], parts[:, first, 2:4],
                                            ALU.add).then_inc(sum_step, 1)
                    wait(pool, sum_step, n + 4)
                    nc.gpsimd.tensor_tensor(parts[:, first, 0], parts[:, first, 0], parts[:, first, 1],
                                            ALU.add).then_inc(sum_step, 1)
                    wait(pool, sum_step, n + 5)
                    plain(pool)
                    nc.gpsimd.tensor_tensor(rows(x_all, g, b), rows(x_all, g, b), parts[:, first, 0],
                                            ALU.add).then_inc(sum_step, 1)

                for s in range(E):
                    for g, e in z_work(i, s):
                        if e < EARLY:
                            z_low(g, e)
                    if s < 8 and has(gd):
                        sum_pairs(gd, 8 + s)
                    if s >= 9 and has(gc):
                        sum_pairs(gc, s - 9)
                    if s == 8 and has(gc):
                        wait(pool, rsum_c_done, gc + 1)
                        if isinstance(i, int):
                            pool.wait_ge(prep_dve, 6)
                        plain(pool)
                        nc.gpsimd.tensor_scalar(rs_c[:], rsum_c[:], out_scale[:], None,
                                                ALU.mult).then_inc(rs_c_done, 1)
                        wait(pool, rs_c_done, gc + 1)
                        wait(pool, y_scaled, 4 * G * gc)
                        plain(pool)
                        nc.gpsimd.tensor_tensor(w_out[:], w_all[:, bass.ds(G * gc, G), :],
                                                rs_c[:].unsqueeze(2).broadcast_to([P, G, E]),
                                                ALU.mult).then_inc(w_out_done, 1)
                    if s == 11 and has(g1 + 1):
                        first_rstd(g1 + 1)
                    if s == 4 and isinstance(i, int) and i == -2:
                        setup_norms()
                    if s == 13 and isinstance(i, int) and i == -2:
                        setup_max()
                if has(g1):
                    second_rstd(g1)
                if has(gc):
                    sum_pairs(gc, 7)

            passes(pool, body)

        @block.scalar
        def _(act):
            act.wait_ge(small_in, 16 * 7)
            nc.scalar.activation(tanh_x[:], gx[:], ACT.Tanh)
            nc.scalar.activation(tanh_f[:], gf[:], ACT.Tanh)
            nc.scalar.activation(sig[:], gates_b[:], ACT.Sigmoid).then_inc(tanh_done, 1)
            act.wait_ge(tanh_done, 1)
            act.wait_ge(prep_pe, 2)
            nc.scalar.activation(m_qk[:], acc_p[Q][:, 0:P], ACT.Copy)
            nc.scalar.activation(wvT[:], acc_p[K][:, 0:P], ACT.Copy, scale=tanh_x[:]).then_inc(tanh_done, 1)

            def weight_high(m):
                act.wait_ge(prep_dve, 5)
                nc.scalar.activation(w_hi[:, m], stage[:, m], ACT.Copy, scale=w_up[:, m:m + 1]).then_inc(hi_done, 1)

            def z_high(g, e):
                wait(act, z_full_done, E * g + e + 1)
                wait(act, expert_used, E * (g - 1) + e + 1)
                nc.scalar.activation(z[:, 0, e, :], z_full[:, e % Z_SLOTS, :], ACT.Copy).then_inc(z_hi_done, 1)

            def body(i):
                g1, g2, gc = i + 2, i + 1, i - 1
                for s in range(E):
                    if s == E - 1 and has(i):
                        wait(act, cscore_ps, i)
                        wait(act, v_ps, i)
                        for m, dst in enumerate((qT, kT, vT)):
                            wait(act, acc_ps[m], i + 1)
                            nc.scalar.activation(dst[:], acc_p[m][:], ACT.Copy,
                                                 scale=1.0 / (X_UP * W_UP)).then_inc(acc_sb[m], 1)
                    if s == 2 and has(gc):
                        wait(act, cmax_done, 2 * gc + 2)
                        wait(act, cpT_ps, gc)
                        wait(act, rsum_c_done, gc)
                        for b in range(G):
                            last = nc.scalar.activation(pc[:, b, :], m1[:, tok(b)], ACT.Exp,
                                                        bias=nmax_c[:, b:b + 1], scale=score_scale[:],
                                                        accum_out=sum_c[:, b:b + 1])
                        last.then_inc(cexp_done, 1)
                    for g, e in z_work(i, s):
                        z_high(g, e)
                    if s == 0 and has(gc):
                        wait(act, v_ps, gc + 1)
                        wait(act, oT_ps, gc)
                        nc.scalar.activation(v_sb[:].rearrange("p b h -> p (b h)"), m0[:],
                                             ACT.Copy).then_inc(v_tok_sb, 1)
                    if s == 2 and has(g2):
                        wait(act, x2T_ps, g2 + 1)
                        wait(act, z_full_done, E * g2)
                        nc.scalar.activation(x2T[:], m0[:], ACT.Copy, scale=X_UP).then_inc(x2T_sb, 1)
                    if s in (3, 6, 8, 10) and isinstance(i, int) and i == -1:
                        weight_high((3, 6, 8, 10).index(s))
                    if s == 3 and has(g1):
                        wait(act, xnT_ps, g1 + 1)
                        wait(act, qxT_ps, g1)
                        nc.scalar.activation(xnT[:], m1[:], ACT.Copy).then_inc(xnT_sb, 1)
                    if s == 5 and has(g2):
                        wait(act, gate_arg_done, g2 + 1)
                        nc.scalar.activation(gate_e[:], gate_arg[:], ACT.Exp).then_inc(gate_exp, 1)
                    if s == 5 and has(gc):
                        wait(act, cpT_ps, gc + 1)
                        wait(act, oT_ps, gc)
                        nc.scalar.activation(pcT[:], m1[:], ACT.Copy).then_inc(cpT_sb, 1)
                    if s == 6 and has(g1):
                        wait(act, qxT_ps, g1 + 1)
                        wait(act, xscore_ps, g1)
                        nc.scalar.activation(qxT[:], m0[:], ACT.Copy, scale=RSQRT_C).then_inc(qxT_sb, 1)
                        wait(act, ctxT_ps, g1 + 1)
                        wait(act, vx_ps, g1)
                        nc.scalar.activation(ctxT[:], m1[:, 0:G * S], ACT.Copy).then_inc(ctxT_sb, 1)
                    if s == 7 and has(g2):
                        wait(act, wT_ps, g2 + 1)
                        wait(act, wb_ps, E * g2)
                        nc.scalar.activation(w_splitT[:], m1[0:2 * E, 0:N // 2].bitcast(F16),
                                             ACT.Copy).then_inc(wT_sb, 1)
                    if s == 8 and has(gc):
                        wait(act, oT_ps, gc + 1)
                        wait(act, y_ps, 4 * G * gc)
                        nc.scalar.activation(o_hi[:], m0[:], ACT.Copy).then_inc(o_hi_done, 1)
                    if s == 9 and has(g1):
                        wait(act, xmax_done, g1 + 1)
                        wait(act, pxT_ps, g1)
                        wait(act, rsum_x_done, g1)
                        for b in range(G):
                            last = nc.scalar.activation(px[:, b, :], m1[:, b * S:(b + 1) * S], ACT.Exp,
                                                        bias=nmax_x[:, b:b + 1],
                                                        accum_out=sum_x[:, b:b + 1])
                        last.then_inc(xexp_done, 1)
                    if s == 10 and has(g1):
                        wait(act, vx_ps, g1 + 1)
                        wait(act, att_ps, g1)
                        nc.scalar.activation(vx[:], m0[0:S, :], ACT.Copy).then_inc(vx_sb, 1)
                    if s == 12 and has(g1):
                        wait(act, pxT_ps, g1 + 1)
                        nc.scalar.activation(pxT[:], m1[0:S, :], ACT.Copy).then_inc(pxT_sb, 1)
            passes(act, body)

        @block.vector
        def _(dve):
            def stats(g, src, bn, mv, done):
                plain(dve)
                for b in range(G):
                    last = nc.vector.bn_stats(bn[:, b, :], rows(src, g, b))
                last.then_inc(done, 1)
                wait(dve, done, 2 * g + 1)
                plain(dve)
                for b in range(G):
                    last = nc.vector.bn_aggr(mv[:, b, :], bn[:, b, :])
                last.then_inc(done, 1)

            def setup():
                dve.wait_ge(small_in, 16 * 7)
                nc.vector.tensor_tensor(sim_sq[:], sim_sb[:], sim_sb[:], ALU.mult).then_inc(prep_dve, 1)
                dve.wait_ge(consts, 1)
                nc.vector.tensor_copy(iota_f[:], iota_i[:]).then_inc(prep_dve, 1)
                dve.wait_ge(prep_pe, 3)
                nc.vector.tensor_copy(sim_sq[:], acc_p[V][:, 0:E]).then_inc(prep_dve, 1)

            def weight_max(m):
                dve.wait_ge(proj_in[m], 16)
                nc.vector.tensor_reduce(wmax[:, m:m + 1], stage[:, m].rearrange("p e h -> p (e h)"), AX_X,
                                        ALU.max, apply_absolute_value=True).then_inc(wmax_done, 1)

            def setup_weights():
                dve.wait_ge(nrm_root, 1)
                step = prep_chain
                nc.vector.tensor_scalar(sim_nrm[:], sim_nrm[:], 1e-12, None, ALU.max).then_inc(step, 1)
                dve.wait_ge(step, 1)
                nc.vector.reciprocal(sim_nrm[:], sim_nrm[:]).then_inc(step, 1)
                dve.wait_ge(step, 2)
                nc.vector.tensor_tensor(sn[:], sim_sb[:], sim_nrm[:], ALU.mult).then_inc(prep_dve, 1)
                dve.wait_ge(wmax_shared, 1)
                nc.vector.tensor_scalar(wmax_all[:], wmax_all[:], 2.0 ** -60, 2.0 ** 60, ALU.max,
                                        ALU.min).then_inc(step, 1)
                dve.wait_ge(step, 3)
                nc.vector.tensor_scalar(w_pow[:].bitcast(U32), wmax_all[:].bitcast(U32), 0x7F800000, None,
                                        ALU.bitwise_and).then_inc(step, 1)
                dve.wait_ge(step, 4)
                nc.vector.reciprocal(w_up[:], w_pow[:]).then_inc(step, 1)
                nc.vector.tensor_scalar(score_scale[:], w_pow[:, Q:Q + 1], w_pow[:, K:K + 1], RSQRT_C,
                                        ALU.mult, ALU.mult)
                nc.vector.tensor_scalar(out_scale[:], w_pow[:, V:V + 1], w_pow[:, O:O + 1], 1.0 / W_UP,
                                        ALU.mult, ALU.mult).then_inc(step, 1)
                dve.wait_ge(step, 6)
                nc.vector.tensor_scalar(w_up[:], w_up[:], W_UP, None, ALU.mult).then_inc(prep_dve, 1)
                dve.wait_ge(tanh_done, 1)
                nc.vector.tensor_scalar(out_scale[:], out_scale[:], tanh_f[:], None, ALU.mult).then_inc(prep_dve, 1)

            def weight_low(m):
                dve.wait_ge(hi_done, m + 1)
                nc.vector.scalar_tensor_tensor(
                    out=w_lo[:, m].rearrange("p e h -> p (e h)"), in0=stage[:, m].rearrange("p e h -> p (e h)"),
                    scalar=w_up[:, m:m + 1], in1=w_hi[:, m].rearrange("p e h -> p (e h)"),
                    op0=ALU.mult, op1=ALU.subtract).then_inc(lo_done, 1)

            def gate_logits(g):
                def link(ins, n):
                    ins.then_inc(gate_step, 1)
                    dve.wait_ge(gate_step, GATE_STEPS * g + n)

                wait(dve, logit_ps, g + 1)
                lg = m0[:, 0:G * E].rearrange("p (b e) -> p b e", e=E)
                link(nc.vector.tensor_tensor(logit[:], lg, rnorm2[:].unsqueeze(2).broadcast_to([P, G, E]),
                                             ALU.mult), 1)
                link(nc.vector.tensor_tensor(logit[:], logit[:], sig[:].unsqueeze(1).broadcast_to([P, G, E]),
                                             ALU.subtract), 2)
                plain(dve)
                for b in range(G):
                    last = nc.vector.max(top[:, b, :], logit[:, b, :])
                last.then_inc(gate_step, 1)

            def gate_mask(g):
                def link(ins, n):
                    ins.then_inc(gate_step, 1)
                    dve.wait_ge(gate_step, GATE_STEPS * g + n)

                dve.wait_ge(gate_step, GATE_STEPS * g + 3)
                plain(dve)
                for b in range(G):
                    nc.vector.max_index(top_at[:, b, :], top[:, b, :], logit[:, b, :])
                nc.vector.tensor_scalar(inactive[:], top[:, :, 0], 0.0, None, ALU.is_le)
                link(nc.vector.tensor_scalar(gate_max[:], top[:, :, 0], 0.0, None, ALU.max), 4)
                nc.vector.scalar_tensor_tensor(out=gate_arg[:], in0=logit[:], scalar=0.0,
                                               in1=gate_max[:].unsqueeze(2).broadcast_to([P, G, E]),
                                               op0=ALU.max, op1=ALU.subtract).then_inc(gate_arg_done, 1)
                iota_b = iota_f[:].unsqueeze(1).broadcast_to([P, G, E])
                nc.vector.tensor_tensor(fb0[:], iota_b, top_at[:, :, 0:1].broadcast_to([P, G, E]), ALU.is_equal)
                link(nc.vector.tensor_tensor(fb1[:], iota_b, top_at[:, :, 1:2].broadcast_to([P, G, E]),
                                             ALU.is_equal), 5)
                link(nc.vector.tensor_tensor(fb0[:], fb0[:], fb1[:], ALU.add), 6)
                link(nc.vector.tensor_tensor(fb0[:], fb0[:], inactive[:].unsqueeze(2).broadcast_to([P, G, E]),
                                             ALU.mult), 7)
                link(nc.vector.scalar_tensor_tensor(out=mask[:], in0=logit[:], scalar=0.0, in1=fb0[:],
                                                    op0=ALU.is_gt, op1=ALU.add), EXP_AT)

            def gate_softmax(g):
                def link(ins, n):
                    ins.then_inc(gate_step, 1)
                    dve.wait_ge(gate_step, GATE_STEPS * g + n)

                w_g = w_all[:, bass.ds(G * g, G), :]
                wait(dve, gate_exp, g + 1)
                link(nc.vector.tensor_tensor(mask[:], gate_e[:], mask[:], ALU.mult), EXP_AT + 1)
                link(nc.vector.reduce_sum(wsum[:], mask[:], AX_X), EXP_AT + 2)
                link(nc.vector.reciprocal(wsum[:], wsum[:]), EXP_AT + 3)
                link(nc.vector.tensor_tensor(w_g, mask[:], wsum[:].unsqueeze(2).broadcast_to([P, G, E]),
                                             ALU.mult), EXP_AT + 4)
                wait(dve, wT_ps, g)
                plain(dve)
                link(nc.vector.tensor_copy(w_split[:, :, 0:E], w_g), EXP_AT + 5)
                nc.vector.tensor_tensor(w_split[:, :, E:2 * E], w_g, w_split[:, :, 0:E],
                                        ALU.subtract).then_inc(w_ready, 1)

            def z_scale(g, e):
                n = E * g + e
                wait(dve, wb_ps, n + 1)
                if e >= Z_SLOTS:
                    wait_low(dve, g, e - Z_SLOTS)
                else:
                    wait_low(dve, g - 1, E + e - Z_SLOTS)
                nc.vector.tensor_tensor(z_full[:, e % Z_SLOTS, :], wb_p[:], x2T[:],
                                        ALU.mult).then_inc(z_full_done, 1)

            def z_low(g, e):
                wait(dve, z_hi_done, E * g + e + 1)
                nc.vector.tensor_tensor(z[:, 1, e, :], z_full[:, e % Z_SLOTS, :], z[:, 0, e, :],
                                        ALU.subtract).then_inc(lo_dve, 1)

            def scale_outputs(g, k):
                b, q = divmod(k, E // 4)
                slot = k % SUM_SLOTS
                wait(dve, y_ps, 4 * G * g + k + 1)
                if k == 0:
                    wait(dve, w_out_done, g + 1)
                if q == 0:
                    wait(dve, sum_step, SUM_STEPS * (G * g + b - 1))
                nc.vector.tensor_tensor(parts[:, slot], y_p[k % 2][:].rearrange("p (e c) -> p e c", e=4),
                                        w_out[:, b, 4 * q:4 * q + 4].unsqueeze(2).broadcast_to([P, 4, P]),
                                        ALU.mult).then_inc(y_scaled, 1)

            def normed(g, dst, mv, rstd, done):
                for b in range(G):
                    last = nc.vector.tensor_scalar(dst[:, b, :], rows(x_all, g, b), mv[:, b, 0:1],
                                                   rstd[:, b:b + 1], ALU.subtract, ALU.mult)
                last.then_inc(done, 1)

            def first_stats(g):
                if isinstance(g, int):
                    dve.wait_ge(x_in[g * G // CHUNK], 16)
                wait(dve, rstd1_done, 2 * g)
                stats(g, x_all, bn1, mv1, bn1_done)

            def body(i):
                g1, g2, gc, gd = i + 2, i + 1, i - 1, i - 2
                first, second = isinstance(i, int) and i == -2, isinstance(i, int) and i == -1
                if first:
                    first_stats(0)
                    setup()
                for s in range(E):
                    zs = z_work(i, s)
                    for g, e in zs[:-1]:
                        z_scale(g, e)
                    if s < 8 and has(gd):
                        scale_outputs(gd, 8 + s)
                    if s >= 9 and has(gc):
                        scale_outputs(gc, s - 9)
                    if s == 2 and has(g1):
                        wait(dve, rstd1_done, 2 * g1 + 2)
                        wait(dve, xnT_ps, g1)
                        normed(g1, xn, mv1, rstd1, xn_done)
                    for g, e in zs[-1:]:
                        z_scale(g, e)
                    if s == 0 and has(g2):
                        wait(dve, rstd2_done, 2 * g2 + 2)
                        wait(dve, x2T_ps, g2)
                        normed(g2, x2, mv2, rstd2, x2_done)
                    if s == 1 and has(gc):
                        wait(dve, cscore_ps, gc + 1)
                        wait(dve, cexp_done, gc)
                        nc.vector.tensor_reduce(nmax_c[:], m1[:].rearrange("p (b t) -> p b t", b=G), AX_X,
                                                ALU.max, negate=True).then_inc(cmax_done, 1)
                        wait(dve, cmax_done, 2 * gc + 1)
                        nc.vector.tensor_scalar(nmax_c[:], nmax_c[:], score_scale[:], None,
                                                ALU.mult).then_inc(cmax_done, 1)
                    if s == 3 and has(g2):
                        wait(dve, norm_step, 2 * g2 + 2)
                        nc.vector.tensor_scalar(rnorm2[:], norm2[:], 1e-12, X_UP, ALU.max,
                                                ALU.mult).then_inc(rnorm_done, 1)
                        wait(dve, rnorm_done, g2 + 1)
                        nc.vector.reciprocal(rnorm2[:], rnorm2[:]).then_inc(rnorm_inv, 1)
                    if s == 4 and has(g2):
                        wait(dve, rnorm_inv, g2 + 1)
                        gate_logits(g2)
                    if s == 5 and has(gc):
                        wait(dve, cexp_done, gc + 1)
                        wait(dve, rs_c_done, gc)
                        nc.vector.reciprocal(rsum_c[:], sum_c[:]).then_inc(rsum_c_done, 1)
                    if s == 5 and has(g2):
                        gate_mask(g2)
                    if s == 6 and has(g2):
                        gate_softmax(g2)
                    if s == 8 and has(gc):
                        wait(dve, o_hi_done, gc + 1)
                        nc.vector.tensor_tensor(o_lo[:], m0[:], o_hi[:], ALU.subtract).then_inc(o_lo_done, 1)
                    if s == 9 and has(g1):
                        wait(dve, xscore_ps, g1 + 1)
                        wait(dve, xexp_done, g1)
                        nc.vector.tensor_reduce(nmax_x[:], m1[:, 0:G * S].rearrange("p (b t) -> p b t", b=G),
                                                AX_X, ALU.max, negate=True).then_inc(xmax_done, 1)
                    if s == 10 and has(g1 + 1):
                        first_stats(g1 + 1)
                    if s == 12 and has(g1):
                        wait(dve, xexp_done, g1 + 1)
                        nc.vector.reciprocal(rsum_x[:], sum_x[:]).then_inc(rsum_x_done, 1)
                    if s == 14 and has(g1):
                        wait(dve, att_ps, g1 + 1)
                        wait(dve, rsum_x_done, g1 + 1)
                        for b in range(G):
                            last = nc.vector.scalar_tensor_tensor(
                                out=rows(x_all, g1, b), in0=m0[:, tok(b)], scalar=rsum_x[:, b:b + 1],
                                in1=rows(x_all, g1, b), op0=ALU.mult, op1=ALU.add)
                        last.then_inc(x1_done, 1)
                    if s == 15 and has(g1):
                        wait(dve, x1_done, g1 + 1)
                        wait(dve, norm_step, 2 * g1)
                        stats(g1, x_all, bn2, mv2, bn2_done)
                    for g, e in zs:
                        if e >= EARLY:
                            z_low(g, e)
                    if s in (2, 3, 10, 12) and first:
                        weight_max((2, 3, 10, 12).index(s))
                    if s == 15 and first:
                        setup_weights()
                    if s in (8, 10, 12, 14) and second:
                        weight_low((8, 10, 12, 14).index(s))
                if has(gc):
                    scale_outputs(gc, 7)

            passes(dve, body, x_in)

        @block.tensor
        def _(pe):
            pe.wait_ge(small_in, 16 * 7)
            pe.wait_ge(consts, 1)
            nc.tensor.matmul(acc_p[Q][:, 0:P], wq_sb[:], wk_sb[:], start=True, stop=True).then_inc(prep_pe, 1)
            nc.tensor.transpose(acc_p[K][:, 0:P], wv_sb[:], ident[:]).then_inc(prep_pe, 1)
            pe.wait_ge(prep_dve, 1)
            nc.tensor.matmul(acc_p[V][:, 0:E], ones[:], sim_sq[:], start=True, stop=True).then_inc(prep_pe, 1)

            def broadcast_weights(g, e):
                n = E * g + e
                if e == 0:
                    wait(pe, wT_sb, g + 1)
                wait(pe, z_full_done, n)
                nc.tensor.matmul(wb_p[:], sel[:, e, :], w_splitT[:], start=True, stop=True).then_inc(wb_ps, 1)

            def out_chunk(g, k):
                b, q = divmod(k, E // 4)
                if k == 0:
                    wait(pe, o_lo_done, g + 1)
                    if isinstance(g, int) and g == 0:
                        pe.wait_ge(lo_done, 4)
                wait(pe, y_scaled, 4 * G * g + k - 1)
                for n, (lhs, rhs) in enumerate(((o_hi, w_hi), (o_hi, w_lo), (o_lo, w_hi))):
                    last = nc.tensor.matmul(y_p[k % 2][:], lhs[:, tok(b)],
                                            rhs[:, O, 4 * q:4 * q + 4, :].rearrange("p e h -> p (e h)"),
                                            start=(n == 0), stop=(n == 2))
                last.then_inc(y_ps, 1)

            def body(i):
                g1, g2, gc, gd = i + 2, i + 1, i - 1, i - 2
                for s in range(E):
                    zs = z_work(i, s)
                    if has(i):
                        if isinstance(i, int) and i == 0 and s == 0:
                            pe.wait_ge(lo_done, 3)
                        wait_low(pe, i, s)
                        for m in (Q, K, V):
                            if s == 0:
                                wait(pe, acc_sb[m], i)
                            for n, (w, half) in enumerate(((w_hi, 0), (w_lo, 0), (w_hi, 1))):
                                last = nc.tensor.matmul(acc_p[m][:], w[:, m, s, :], z[:, half, s, :],
                                                        start=(s == 0 and n == 0), stop=(s == E - 1 and n == 2))
                            if s == E - 1:
                                last.then_inc(acc_ps[m], 1)
                            if m == K:
                                for g, e in zs[:-1]:
                                    broadcast_weights(g, e)
                        if s < E - 1:
                            last.then_inc(expert_used, 1)
                        else:
                            pe.sem_inc(expert_used, 1)
                    else:
                        for g, e in zs[:-1]:
                            broadcast_weights(g, e)
                    if s < 8 and has(gd):
                        out_chunk(gd, 8 + s)
                    if s >= 9 and has(gc):
                        out_chunk(gc, s - 9)
                    for g, e in zs[-1:]:
                        broadcast_weights(g, e)
                    if s == 0 and has(gc):
                        wait(pe, acc_sb[V], gc + 1)
                        wait(pe, x1_done, cap(i + 2))
                        if isinstance(i, int):
                            wait(pe, o_lo_done, gc)
                        for b in range(G):
                            last = nc.tensor.transpose(m0[:, tok(b)], vT[:, tok(b)], ident[:])
                        last.then_inc(v_ps, 1)
                    if s == 1 and has(gc):
                        wait(pe, acc_sb[K], gc + 1)
                        wait(pe, pxT_sb, cap(i + 2))
                        for b in range(G):
                            last = nc.tensor.matmul(m1[:, tok(b)], qT[:, tok(b)], kT[:, tok(b)],
                                                    start=True, stop=True)
                        last.then_inc(cscore_ps, 1)
                    if s == 2 and has(g2):
                        wait(pe, x2_done, g2 + 1)
                        wait(pe, v_tok_sb, cap(i))
                        for b in range(G):
                            last = nc.tensor.transpose(m0[:, tok(b)], x2[:, b, :], ident[:])
                        last.then_inc(x2T_ps, 1)
                    if s == 3 and has(g1):
                        wait(pe, xn_done, g1 + 1)
                        wait(pe, cexp_done, cap(i))
                        for b in range(G):
                            last = nc.tensor.transpose(m1[:, tok(b)], xn[:, b, :], ident[:])
                        last.then_inc(xnT_ps, 1)
                    if s == 4 and has(g2):
                        if isinstance(i, int) and i == -1:
                            pe.wait_ge(prep_dve, 4)
                        wait(pe, x2T_sb, g2 + 1)
                        for b in range(G):
                            last = nc.tensor.matmul(m0[:, b * E:(b + 1) * E], x2T[:, tok(b)], sn[:],
                                                    start=True, stop=True)
                        last.then_inc(logit_ps, 1)
                    if s == 5 and has(gc):
                        wait(pe, cexp_done, gc + 1)
                        wait(pe, xnT_sb, cap(i + 3))
                        for b in range(G):
                            last = nc.tensor.transpose(m1[:, tok(b)], pc[:, b, :], ident[:])
                        last.then_inc(cpT_ps, 1)
                    if s == 6 and has(g1):
                        if isinstance(i, int) and i == -2:
                            pe.wait_ge(tanh_done, 2)
                        wait(pe, xnT_sb, g1 + 1)
                        if not (isinstance(i, int) and i == -2):
                            wait(pe, gate_step, GATE_STEPS * (i + 1) + 1)
                        nc.tensor.matmul(m0[:], m_qk[:], xnT[:], start=True, stop=True).then_inc(qxT_ps, 1)
                        wait(pe, ctx_loaded, 16 * g1 + 16)
                        wait(pe, cpT_sb, cap(i))
                        for b in range(G):
                            last = nc.tensor.transpose(m1[:, b * S:(b + 1) * S], ctx_g[:, b, :],
                                                       ident[0:S, 0:S])
                        last.then_inc(ctxT_ps, 1)
                    if s == 7 and has(g2):
                        wait(pe, w_ready, g2 + 1)
                        wait(pe, ctxT_sb, cap(i + 3))
                        if isinstance(i, int):
                            wait(pe, cpT_sb, cap(i))
                        for b in range(G):
                            last = nc.tensor.transpose(m1[0:2 * E, b * P // 2:(b + 1) * P // 2].bitcast(F16),
                                                       w_split[:, b, :], ident16[:])
                        last.then_inc(wT_ps, 1)
                    if s == 8 and has(gc):
                        wait(pe, v_tok_sb, gc + 1)
                        wait(pe, cpT_sb, gc + 1)
                        wait(pe, qxT_sb, cap(i + 3))
                        if isinstance(i, int):
                            wait(pe, gate_step, GATE_STEPS * (cap(i + 2) - 1) + 1)
                        for b in range(G):
                            last = nc.tensor.matmul(m0[:, tok(b)], v_sb[:, b, :], pcT[:, tok(b)],
                                                    start=True, stop=True)
                        last.then_inc(oT_ps, 1)
                    if s == 9 and has(g1):
                        wait(pe, qxT_sb, g1 + 1)
                        wait(pe, ctxT_sb, g1 + 1)
                        wait(pe, wT_sb, cap(i + 2))
                        for b in range(G):
                            last = nc.tensor.matmul(m1[:, b * S:(b + 1) * S], qxT[:, tok(b)],
                                                    ctxT[:, b * S:(b + 1) * S], start=True, stop=True)
                        last.then_inc(xscore_ps, 1)
                    if s == 10 and has(g1):
                        wait(pe, o_lo_done, cap(i))
                        for b in range(G):
                            last = nc.tensor.matmul(m0[0:S, tok(b)], ctxT[:, b * S:(b + 1) * S], wvT[:],
                                                    start=True, stop=True)
                        last.then_inc(vx_ps, 1)
                    if s == 12 and has(g1):
                        wait(pe, xexp_done, g1 + 1)
                        for b in range(G):
                            last = nc.tensor.transpose(m1[0:S, tok(b)], px[:, b, :], ident[:])
                        last.then_inc(pxT_ps, 1)
                    if s == 14 and has(g1):
                        wait(pe, pxT_sb, g1 + 1)
                        wait(pe, vx_sb, g1 + 1)
                        for b in range(G):
                            last = nc.tensor.matmul(m0[:, tok(b)], pxT[:, tok(b)], vx[:, tok(b)],
                                                    start=True, stop=True)
                        last.then_inc(att_ps, 1)
                if has(gc):
                    out_chunk(gc, 7)

            passes(pe, body)


_INS = ['x', 'ctx_1024', 'g_xattn', 'g_ffn', 'L0_xattn_Wk', 'L0_xattn_Wq', 'L0_xattn_Wv', 'L0_ffn_sim_matrix',
        'L0_ffn_gates', 'L0_ffn_q_proj', 'L0_ffn_k_proj', 'L0_ffn_v_proj', 'L0_ffn_o_proj']


def kernel(**inputs):
    import numpy as _np
    import concourse.bacc as _bacc
    from concourse import mybir as _mybir
    from concourse.bass_utils import run_bass_kernel_spmd as _run

    nc = _bacc.Bacc("TRN2", target_bir_lowering=False, num_devices=1)
    arrays, args = {}, []
    for name in _INS:
        a = _np.ascontiguousarray(inputs[name])
        arrays[f"in_{name}_dram"] = a
        args.append(nc.dram_tensor(f"in_{name}_dram", a.shape, _mybir.dt.from_np(a.dtype), kind="ExternalInput").ap())
    out = nc.dram_tensor("out_dram", arrays["in_x_dram"].shape, _mybir.dt.float32, kind="ExternalOutput").ap()
    flamingo_gated_moe_attention(nc, *args, out)
    r = _run(nc, [arrays], core_ids=[0])
    return r.results[0]["out_dram"]
```

```python
from contextlib import ExitStack

import concourse.bass as bass
from concourse import mybir

ALU = mybir.AluOpType
ACT = mybir.ActivationFunctionType
F32 = mybir.dt.float32
F16 = mybir.dt.float16
U32 = mybir.dt.uint32
I32 = mybir.dt.int32
AX_X = mybir.AxisListType.X
ABSMAX = bass.bass_isa.ReduceOp.absmax

P = 128
G = 4
Q, K, V, O = range(4)
EPS = 1e-5
X_UP = 4096.0
W_UP = 16384.0
W_SLOTS = 4
Z_SLOTS = 4
SUM_SLOTS = 8
SUM_STEPS = 6
GATE_STEPS = 12
EXP_AT = 8


Z_LATE = {0: (7,), 1: (8,), 2: (9,), 3: (10,), 4: (11,), 5: (12,), 6: (13,), 7: (14,), 8: (15,)}
Z_EARLY = {10: (0,), 11: (1,), 12: (2,), 13: (3, 4), 14: (5,), 15: (6,)}

EARLY = 10


def flamingo_gated_moe_attention(nc, x, ctx_in, g_xattn, g_ffn, Wk, Wq, Wv, sim_matrix, gates,
                                 q_proj, k_proj, v_proj, o_proj, out):
    B, T, C = x.shape
    _, S, _ = ctx_in.shape
    E = sim_matrix.shape[1]
    assert T == P and C == P and E == 16 and B % G == 0
    NG = B // G
    N = G * P
    LOOP = (3, NG - 3)
    X_LOADS = [0, G] + [c * B // 4 for c in range(1, 5)]
    RSQRT_C = float(P) ** -0.5

    with ExitStack() as ctx:
        def sb(name, shape, dt=F32):
            return ctx.enter_context(nc.sbuf_tensor(name, shape, dt))

        def psum(name):
            return ctx.enter_context(nc.psum_tensor(name, [P, N], F32))

        def sem(name):
            return ctx.enter_context(nc.semaphore(name))

        x_all = sb("x_all", [P, B, C])
        ctx_g = sb("ctx_g", [S, G, C])
        w_hi = sb("w_hi", [P, 4, E, P], F16)
        w_lo = sb("w_lo", [P, 4, E, P], F16)
        w_all = sb("w_all", [P, B, E])
        z = sb("z", [P, 2, E, N], F16)
        stage = sb("stage", [P, 4, E, P])
        z_full = sb("z_full", [P, Z_SLOTS, N])
        ident = sb("ident", [P, P])
        ones = sb("ones", [P, P])
        iota_i = sb("iota_i", [P, E], I32)
        iota_f = sb("iota_f", [P, E])
        minus_half = sb("minus_half", [P, G])
        plus_half = sb("plus_half", [P, E])
        gx = sb("gx", [P, 1])
        gf = sb("gf", [P, 1])
        tanh_x = sb("tanh_x", [P, 1])
        tanh_f = sb("tanh_f", [P, 1])
        gates_b = sb("gates_b", [P, E])
        sig = sb("sig", [P, E])
        sim_sb = sb("sim_sb", [P, E])
        sim_sq = sb("sim_sq", [P, E])
        sim_nrm = sb("sim_nrm", [P, E])
        sn = sb("sn", [P, E])
        wk_sb = sb("wk_sb", [P, P])
        wq_sb = sb("wq_sb", [P, P])
        wv_sb = sb("wv_sb", [P, P])
        m_kq = sb("m_kq", [P, P])
        wvT = sb("wvT", [P, P])
        wmax = sb("wmax", [P, 4])
        wmax_all = sb("wmax_all", [P, 4])
        w_pow = sb("w_pow", [P, 4])
        w_up = sb("w_up", [P, 4])
        score_scale = sb("score_scale", [P, 1])
        out_scale = sb("out_scale", [P, 1])
        bn1 = sb("bn1", [P, G, 6])
        mv1 = sb("mv1", [P, G, 2])
        rstd1 = sb("rstd1", [P, G])
        xn = sb("xn", [P, G, C])
        xnT = sb("xnT", [P, N])
        ctxT = sb("ctxT", [P, G * S])
        kxT = sb("kxT", [P, G * S])
        nmax_x = sb("nmax_x", [P, G])
        px = sb("px", [P, G, S])
        sum_x = sb("sum_x", [P, G])
        rsum_x = sb("rsum_x", [P, G])
        pxT = sb("pxT", [S, N])
        vx = sb("vx", [S, N])
        bn2 = sb("bn2", [P, G, 6])
        mv2 = sb("mv2", [P, G, 2])
        rstd2 = sb("rstd2", [P, G])
        norm2 = sb("norm2", [P, G])
        rnorm2 = sb("rnorm2", [P, G])
        x2 = sb("x2", [P, G, C])
        x2T_next = sb("x2T_next", [P, N])
        x2T = sb("x2T", [P, N])
        logit = sb("logit", [P, G, E])
        top = sb("top", [P, G, 8])
        top_at = sb("top_at", [P, G, 8], U32)
        gate_max = sb("gate_max", [P, G])
        inactive = sb("inactive", [P, G])
        gate_arg = sb("gate_arg", [P, G, E])
        gate_e = sb("gate_e", [P, G, E])
        fb0 = sb("fb0", [P, G, E])
        fb1 = sb("fb1", [P, G, E])
        mask = sb("mask", [P, G, E])
        wsum = sb("wsum", [P, G])
        w_new = sb("w_new", [P, G, E])
        wT = sb("wT", [E, N])
        w_rows = nc.dram_tensor("w_rows", [E, N], F32, kind="Internal").ap()
        w_bc = sb("w_bc", [P, W_SLOTS, 2, N])
        qT = sb("qT", [P, N])
        kT = sb("kT", [P, N])
        vT = sb("vT", [P, N])
        v_sb = sb("v_sb", [P, G, P])
        nmax_c = sb("nmax_c", [P, G])
        pc = sb("pc", [P, G, P])
        sum_c = sb("sum_c", [P, G])
        rsum_c = sb("rsum_c", [P, G])
        rs_c = sb("rs_c", [P, G])
        pcT = sb("pcT", [P, N])
        o_hi = sb("o_hi", [P, N], F16)
        o_lo = sb("o_lo", [P, N], F16)
        w_out = sb("w_out", [P, G, E])
        o_end = [sb("o_end_hi", [P, N], F16), sb("o_end_lo", [P, N], F16)]
        w_out_end = sb("w_out_end", [P, G, E])
        parts = stage[:].rearrange("p m (k e) c -> p (m k) e c", e=4)
        assert parts.shape[1] == 2 * SUM_SLOTS
        acc_p = [psum("acc_q"), psum("acc_k"), psum("acc_v")]
        y_p = [psum("y0"), psum("y1")]
        m0 = psum("m0")
        m1 = psum("m1")
        m2 = psum("m2")

        x_in = [sem(f"x_in{c}") for c in range(len(X_LOADS) - 1)]
        ctx_loaded = sem("ctx_loaded")
        small_in = sem("small_in")
        proj_in = [sem(f"proj_in{m}") for m in range(4)]
        out_stored = sem("out_stored")
        pool_set = sem("pool_set")
        consts = sem("consts")
        passed = sem("passed")
        tanh_done = sem("tanh_done")
        prep_pe = sem("prep_pe")
        prep_dve = sem("prep_dve")
        prep_chain = sem("prep_chain")
        wmax_done = sem("wmax_done")
        wmax_shared = sem("wmax_shared")
        hi_done = sem("hi_done")
        lo_done = sem("lo_done")
        nrm_root = sem("nrm_root")
        bn1_done = sem("bn1_done")
        rstd1_done = sem("rstd1_done")
        xn_done = sem("xn_done")
        xnT_ps = sem("xnT_ps")
        xnT_sb = sem("xnT_sb")
        kxT_ps = sem("kxT_ps")
        kxT_sb = sem("kxT_sb")
        ctxT_ps = sem("ctxT_ps")
        ctxT_sb = sem("ctxT_sb")
        xscore_ps = sem("xscore_ps")
        xmax_done = sem("xmax_done")
        xexp_done = sem("xexp_done")
        vx_ps = sem("vx_ps")
        vx_sb = sem("vx_sb")
        pxT_ps = sem("pxT_ps")
        pxT_sb = sem("pxT_sb")
        att_ps = sem("att_ps")
        rsum_x_done = sem("rsum_x_done")
        x1_done = sem("x1_done")
        bn2_done = sem("bn2_done")
        rstd2_done = sem("rstd2_done")
        norm_step = sem("norm_step")
        rnorm_done = sem("rnorm_done")
        rnorm_inv = sem("rnorm_inv")
        x2_done = sem("x2_done")
        x2T_ps = sem("x2T_ps")
        x2T_sb = sem("x2T_sb")
        x2T_moved = sem("x2T_moved")
        logit_ps = sem("logit_ps")
        gate_step = sem("gate_step")
        gate_arg_done = sem("gate_arg_done")
        gate_exp = sem("gate_exp")
        w_ready = sem("w_ready")
        wT_ps = sem("wT_ps")
        wT_sb = sem("wT_sb")
        w_rows_in = sem("w_rows_in")
        w_bc_in = [sem(f"w_bc_in{k}") for k in range(W_SLOTS)]
        z_full_done = sem("z_full_done")
        z_hi_done = sem("z_hi_done")
        lo_pool = sem("lo_pool")
        lo_dve = sem("lo_dve")
        expert_used = sem("expert_used")
        acc_ps = [sem("q_ps"), sem("k_ps"), sem("v_ps")]
        acc_sb = [sem("q_sb"), sem("k_sb"), sem("vT_sb")]
        v_ps = sem("v_tok_ps")
        v_tok_sb = sem("v_tok_sb")
        cscore_ps = sem("cscore_ps")
        cmax_done = sem("cmax_done")
        cexp_done = sem("cexp_done")
        cpT_ps = sem("cpT_ps")
        cpT_sb = sem("cpT_sb")
        oT_ps = sem("oT_ps")
        o_hi_done = sem("o_hi_done")
        o_lo_done = sem("o_lo_done")
        rsum_c_done = sem("rsum_c_done")
        rs_c_done = sem("rs_c_done")
        w_out_done = sem("w_out_done")
        y_ps = sem("y_ps")
        y_scaled = sem("y_scaled")
        sum_step = sem("sum_step")
        end_scaled = sem("end_scaled")
        end_step = sem("end_step")

        block = ctx.enter_context(nc.Block())

        def wait(eng, s, count):
            if not isinstance(count, int) or count > 0:
                eng.wait_ge(s, count)

        def plain(eng):
            eng.sem_inc(passed, 1)

        def cap(groups):
            return min(groups, NG) if isinstance(groups, int) else groups

        def has(g):
            return not isinstance(g, int) or 0 <= g < NG

        def passes(eng, body, loads=()):
            for i in range(-2, LOOP[0]):
                body(i)
            for load in loads:
                eng.wait_ge(load, 16)
            with eng.Fori(LOOP[0], LOOP[1]) as i:
                body(i)
            for i in range(LOOP[1], NG + 2):
                body(i)

        HIGH_AT = [(-1, 0), (-1, 4), (-1, 7), (0, 10)]
        LOW_AT = [(-1, 3), (-1, 6), (-1, 8), (0, 12)]

        def z_work(i, s):
            late = [(i, e) for e in Z_LATE.get(s, ())] if has(i) else []
            return late + ([(i + 1, e) for e in Z_EARLY.get(s, ())] if has(i + 1) else [])

        END = [(NG - 2, 2), (NG - 1, 0), (NG - 1, 2)]
        END_SCALED = 4 * G * (NG - 2) + 2 * 4
        END_SUMMED = G * (NG - 2) + 2
        end_p = [y_p[0], y_p[1], acc_p[Q], acc_p[K]]
        end_w = [w_out, w_out_end, w_out_end]
        END_SLOTS = [SUM_SLOTS, 0, SUM_SLOTS]

        def end_work(i, s, at):
            if i == NG:
                return [(0, n) for n in at.get(s, ())] + ([(1, s - 9)] if s >= 9 else [])
            return [(2, s)] if i == NG + 1 and s < 8 else []

        END_PE = {2: (0, 1, 2), 3: (3,), 6: (4,), 8: (5, 6, 7)}
        END_ACT = {6: (1,), 9: (3, 5, 7)}
        END_DVE = {2: (0,), 3: (2,), 6: (4,), 8: (3, 5, 6, 7)}

        def wait_low(eng, g, e):
            if e < EARLY:
                wait(eng, lo_pool, EARLY * g + e + 1)
            else:
                wait(eng, lo_dve, (E - EARLY) * g + e - EARLY + 1)

        def rows(t, g, b):
            return t[:, bass.ds(G * g + b, 1), :].rearrange("p a c -> p (a c)")

        def tok(b):
            return slice(b * P, (b + 1) * P)

        @block.sync
        def _(sp):
            x_v = x.rearrange("b n c -> n b c")
            c_v = ctx_in.rearrange("b s c -> s b c")

            def load_x(c):
                seqs = slice(X_LOADS[c], X_LOADS[c + 1])
                sp.dma_start(x_all[:, seqs, :], x_v[:, seqs, :]).then_inc(x_in[c], 16)

            load_x(0)
            for dst, src in ((wq_sb, Wq), (wk_sb, Wk), (wv_sb, Wv), (sim_sb, sim_matrix)):
                sp.dma_start(dst[:], src).then_inc(small_in, 16)
            sp.dma_start(gx[:], g_xattn.partition_broadcast(P)).then_inc(small_in, 16)
            sp.dma_start(gf[:], g_ffn.partition_broadcast(P)).then_inc(small_in, 16)
            sp.dma_start(gates_b[:], gates.partition_broadcast(P)).then_inc(small_in, 16)
            sp.dma_start(ctx_g[:], c_v[:, 0:G, :]).then_inc(ctx_loaded, 16)
            load_x(1)
            for m, w in enumerate((q_proj, k_proj, v_proj, o_proj)):
                sp.dma_start(stage[:, m], w.rearrange("e c h -> c e h")).then_inc(proj_in[m], 16)
            for c in range(2, len(X_LOADS) - 1):
                load_x(c)
            o_v = out.rearrange("b n c -> n b c")

            def load_context(g):
                sp.wait_ge(ctxT_ps, g)
                sp.dma_start(ctx_g[:], c_v[:, bass.ds(G * g, G), :]).then_inc(ctx_loaded, 16)

            def store(g):
                sp.wait_ge(sum_step, G * SUM_STEPS * g + G * SUM_STEPS)
                sp.dma_start(o_v[:, bass.ds(G * g, G), :], x_all[:, bass.ds(G * g, G), :]).then_inc(out_stored, 16)

            def spread_weights(g):
                wait(sp, wT_sb, g + 1)
                plain(sp)
                for k in range(W_SLOTS):
                    wait(sp, w_bc_in[k], 16 * (E // 2 // W_SLOTS) * g)
                    plain(sp)
                sp.dma_start(w_rows, wT[:]).then_inc(w_rows_in, 16)
                wait(sp, w_rows_in, 16 * g + 16)
                plain(sp)
                for j in range(E // 2):
                    wait(sp, z_full_done, E * g + 2 * (j - W_SLOTS + 1))
                    sp.dma_start(w_bc[:, j % W_SLOTS].rearrange("p e n -> p (e n)"),
                                 w_rows[2 * j:2 * j + 2, :].rearrange("e n -> (e n)").partition_broadcast(P)
                                 ).then_inc(w_bc_in[j % W_SLOTS], 16)

            load_context(1)
            for g in range(3):
                load_context(g + 2)
                spread_weights(g)
            with sp.Fori(3, NG - 2) as g:
                load_context(g + 2)
                spread_weights(g)
                store(g - 3)
            for g in range(NG - 2, NG):
                spread_weights(g)
                store(g - 3)
            store(NG - 3)
            for p, (g, b) in enumerate(END):
                sp.wait_ge(sum_step, SUM_STEPS * (END_SUMMED + p + 1))
                sp.wait_ge(end_step, SUM_STEPS * (p + 1))
                first = G * g if p == 0 else G * g + b
                sp.dma_start(o_v[:, first:G * g + b + 2, :],
                             x_all[:, first:G * g + b + 2, :]).then_inc(out_stored, 16)
            sp.wait_ge(out_stored, 16 * (NG + 1))

        @block.gpsimd
        def _(pool):
            nc.gpsimd.memset(ident[:], 0.0).then_inc(pool_set, 1)
            nc.gpsimd.memset(ones[:], 1.0)
            nc.gpsimd.memset(minus_half[:], -0.5)
            nc.gpsimd.memset(plus_half[:], 0.5)
            nc.gpsimd.iota(iota_i[:], pattern=[[1, E]], base=0, channel_multiplier=0).then_inc(pool_set, 1)
            pool.wait_ge(pool_set, 2)
            nc.gpsimd.affine_select(out=ident[:], in_=ident[:], compare_op=ALU.not_equal, fill=1.0, base=0,
                                    pattern=[[-1, P]], channel_multiplier=1).then_inc(consts, 1)

            def setup_norms():
                pool.wait_ge(prep_dve, 3)
                nc.gpsimd.tensor_tensor(sim_nrm[:], sim_sq[:], plus_half[:], ALU.pow).then_inc(nrm_root, 1)

            def setup_max():
                pool.wait_ge(wmax_done, 4)
                nc.gpsimd.partition_all_reduce(wmax_all[:], wmax[:], P, ABSMAX).then_inc(wmax_shared, 1)

            def first_rstd(g):
                wait(pool, bn1_done, 2 * g + 2)
                plain(pool)
                nc.gpsimd.tensor_scalar(rstd1[:], mv1[:, :, 1], EPS, None, ALU.add).then_inc(rstd1_done, 1)
                wait(pool, rstd1_done, 2 * g + 1)
                nc.gpsimd.tensor_tensor(rstd1[:], rstd1[:], minus_half[:], ALU.pow).then_inc(rstd1_done, 1)

            def second_rstd(g):
                wait(pool, bn2_done, 2 * g + 2)
                plain(pool)
                nc.gpsimd.tensor_scalar(rstd2[:], mv2[:, :, 1], EPS, None, ALU.add)
                wait(pool, rnorm_done, g)
                plain(pool)
                nc.gpsimd.tensor_scalar(norm2[:], mv2[:, :, 1], float(C), None, ALU.mult).then_inc(rstd2_done, 1)
                wait(pool, rstd2_done, 2 * g + 1)
                nc.gpsimd.tensor_tensor(rstd2[:], rstd2[:], minus_half[:], ALU.pow).then_inc(rstd2_done, 1)
                nc.gpsimd.tensor_tensor(norm2[:], norm2[:], plus_half[:, 0:G], ALU.pow).then_inc(norm_step, 1)
                wait(pool, norm_step, 2 * g + 1)
                nc.gpsimd.tensor_tensor(norm2[:], norm2[:], rstd2[:], ALU.mult).then_inc(norm_step, 1)

            def body(i):
                g1, g2, gc, gd = i + 2, i + 1, i - 1, i - 2
                if isinstance(i, int) and i == -2:
                    first_rstd(0)

                def z_low(g, e):
                    wait(pool, z_hi_done, E * g + e + 1)
                    nc.gpsimd.tensor_tensor(z[:, 1, e, :], z_full[:, e % Z_SLOTS, :], z[:, 0, e, :],
                                            ALU.subtract).then_inc(lo_pool, 1)

                def sum_pairs(g, k):
                    b, q = divmod(k, E // 4)
                    slot = k % SUM_SLOTS
                    if k in (4, 8, 12):
                        sum_rest(g, b - 1, 4 * (b - 1) % SUM_SLOTS, SUM_STEPS * (G * g + b - 1))
                    if q % 2 == 1:
                        wait(pool, y_scaled, 4 * G * g + k + 1)
                        nc.gpsimd.tensor_tensor(parts[:, slot - 1], parts[:, slot - 1], parts[:, slot],
                                                ALU.add).then_inc(sum_step, 1)
                    if k == 4 * G - 1 or (k == 7 and isinstance(i, int) and i == NG - 1):
                        sum_rest(g, b, 4 * b % SUM_SLOTS, SUM_STEPS * (G * g + b))

                def sum_rest(g, b, first, n):
                    wait(pool, sum_step, n + 2)
                    nc.gpsimd.tensor_tensor(parts[:, first], parts[:, first], parts[:, first + 2],
                                            ALU.add).then_inc(sum_step, 1)
                    sum_slot(g, b, first, n)

                def sum_slot(g, b, first, n):
                    wait(pool, sum_step, n + 3)
                    nc.gpsimd.tensor_tensor(parts[:, first, 0:2], parts[:, first, 0:2], parts[:, first, 2:4],
                                            ALU.add).then_inc(sum_step, 1)
                    wait(pool, sum_step, n + 4)
                    nc.gpsimd.tensor_tensor(parts[:, first, 0], parts[:, first, 0], parts[:, first, 1],
                                            ALU.add).then_inc(sum_step, 1)
                    wait(pool, sum_step, n + 5)
                    plain(pool)
                    nc.gpsimd.tensor_tensor(rows(x_all, g, b), rows(x_all, g, b), parts[:, first, 0],
                                            ALU.add).then_inc(sum_step, 1)

                end = isinstance(i, int) and i >= NG

                def end_sum(pair, n):
                    g, b = END[pair]
                    slot = END_SLOTS[pair]
                    q = n // 2
                    done = SUM_STEPS * (END_SUMMED + pair)
                    if n in (2, 4, 6):
                        pool.wait_ge(y_scaled, END_SCALED + 4 * pair + q + 1)
                        pool.wait_ge(sum_step, done + q - 1)
                        nc.gpsimd.tensor_tensor(parts[:, slot], parts[:, slot], parts[:, slot + q],
                                                ALU.add).then_inc(sum_step, 1)
                    if n == 7:
                        sum_slot(g, b, slot, done)

                for s in range(E):
                    for g, e in z_work(i, s):
                        if e < EARLY:
                            z_low(g, e)
                    if end:
                        for pair, n in end_work(i, s, END_PE):
                            end_sum(pair, n)
                    else:
                        if s < 8 and has(gd):
                            sum_pairs(gd, 8 + s)
                        if s >= 9 and has(gc):
                            sum_pairs(gc, s - 9)
                    if s == (6 if end else 8) and has(gc):
                        wait(pool, rsum_c_done, gc + 1)
                        if isinstance(i, int):
                            pool.wait_ge(prep_dve, 6)
                        plain(pool)
                        nc.gpsimd.tensor_scalar(rs_c[:], rsum_c[:], out_scale[:], None,
                                                ALU.mult).then_inc(rs_c_done, 1)
                        wait(pool, rs_c_done, gc + 1)
                        if not end:
                            wait(pool, y_scaled, 4 * G * gc)
                        plain(pool)
                        nc.gpsimd.tensor_tensor((w_out_end if end else w_out)[:], w_all[:, bass.ds(G * gc, G), :],
                                                rs_c[:].unsqueeze(2).broadcast_to([P, G, E]),
                                                ALU.mult).then_inc(w_out_done, 1)
                    if s == 11 and has(g1 + 1):
                        first_rstd(g1 + 1)
                    if s == 4 and isinstance(i, int) and i == -2:
                        setup_norms()
                    if s == 13 and isinstance(i, int) and i == -2:
                        setup_max()
                if has(g1):
                    second_rstd(g1)
                if end:
                    for pair, n in end_work(i, E, END_PE):
                        end_sum(pair, n)
                elif has(gc):
                    sum_pairs(gc, 7)

            passes(pool, body)

        @block.scalar
        def _(act):
            act.wait_ge(small_in, 16 * 7)
            nc.scalar.activation(tanh_x[:], gx[:], ACT.Tanh)
            nc.scalar.activation(tanh_f[:], gf[:], ACT.Tanh)
            nc.scalar.activation(sig[:], gates_b[:], ACT.Sigmoid).then_inc(tanh_done, 1)
            act.wait_ge(tanh_done, 1)
            act.wait_ge(prep_pe, 2)
            nc.scalar.activation(m_kq[:], acc_p[Q][:, 0:P], ACT.Copy)
            nc.scalar.activation(wvT[:], acc_p[K][:, 0:P], ACT.Copy, scale=tanh_x[:]).then_inc(tanh_done, 1)

            def weight_high(m):
                act.wait_ge(prep_dve, 5)
                nc.scalar.activation(w_hi[:, m], stage[:, m], ACT.Copy, scale=w_up[:, m:m + 1]).then_inc(hi_done, 1)

            def z_high(g, e):
                wait(act, z_full_done, E * g + e + 1)
                wait(act, expert_used, E * (g - 1) + e + 1)
                nc.scalar.activation(z[:, 0, e, :], z_full[:, e % Z_SLOTS, :], ACT.Copy).then_inc(z_hi_done, 1)

            def end_scale(pair, n):
                if n % 2 == 0:
                    return
                g, b = END[pair]
                q = n // 2
                act.wait_ge(y_ps, 4 * G * g + 4 * b + n + 1)
                if n == 1:
                    act.wait_ge(w_out_done, g + 1)
                    if pair == 1:
                        act.wait_ge(sum_step, SUM_STEPS * END_SUMMED)
                    elif pair == 2:
                        act.wait_ge(end_step, SUM_STEPS)
                for j in range(4):
                    last = nc.scalar.activation(parts[:, END_SLOTS[pair] + 4 + q, j, :], end_p[n % 4][:, tok(j)],
                                                ACT.Copy, scale=end_w[pair][:, b + 1, 4 * q + j:4 * q + j + 1])
                last.then_inc(end_scaled, 1)

            def body(i):
                g1, g2, gc = i + 2, i + 1, i - 1
                for s in range(E):
                    if isinstance(i, int) and (i, s) in HIGH_AT:
                        weight_high(HIGH_AT.index((i, s)))
                    if isinstance(i, int) and i >= NG:
                        for pair, n in end_work(i, s, END_ACT):
                            end_scale(pair, n)
                    if s == E - 1 and has(i):
                        wait(act, cscore_ps, i)
                        wait(act, v_ps, i)
                        for m, dst in enumerate((qT, kT, vT)):
                            wait(act, acc_ps[m], i + 1)
                            nc.scalar.activation(dst[:], acc_p[m][:], ACT.Copy,
                                                 scale=1.0 / (X_UP * W_UP)).then_inc(acc_sb[m], 1)
                    if s == 2 and has(gc):
                        wait(act, cmax_done, 2 * gc + 2)
                        wait(act, cpT_ps, gc)
                        wait(act, rsum_c_done, gc)
                        for b in range(G):
                            last = nc.scalar.activation(pc[:, b, :], m1[:, tok(b)], ACT.Exp,
                                                        bias=nmax_c[:, b:b + 1], scale=score_scale[:],
                                                        accum_out=sum_c[:, b:b + 1])
                        last.then_inc(cexp_done, 1)
                    if s == 8 and has(gc):
                        wait(act, oT_ps, gc + 1)
                        if isinstance(i, int) and i == NG:
                            nc.scalar.activation(o_end[0][:], m0[:], ACT.Copy).then_inc(o_hi_done, 1)
                        else:
                            wait(act, y_ps, 4 * G * gc)
                            nc.scalar.activation(o_hi[:], m0[:], ACT.Copy).then_inc(o_hi_done, 1)
                    if s == 0 and has(gc):
                        wait(act, v_ps, gc + 1)
                        wait(act, oT_ps, gc)
                        nc.scalar.activation(v_sb[:].rearrange("p b h -> p (b h)"), m0[:],
                                             ACT.Copy).then_inc(v_tok_sb, 1)
                    if s == 2 and has(g2):
                        wait(act, x2T_ps, g2 + 1)
                        wait(act, x2T_moved, g2)
                        wait(act, logit_ps, g2)
                        nc.scalar.activation(x2T_next[:], m0[:], ACT.Copy, scale=X_UP).then_inc(x2T_sb, 1)
                    if s == 3 and has(g1):
                        wait(act, xnT_ps, g1 + 1)
                        wait(act, xscore_ps, g1)
                        nc.scalar.activation(xnT[:], m1[:], ACT.Copy).then_inc(xnT_sb, 1)
                    if s == 5 and has(g2):
                        wait(act, gate_arg_done, g2 + 1)
                        nc.scalar.activation(gate_e[:], gate_arg[:], ACT.Exp).then_inc(gate_exp, 1)
                    if s == 5 and has(gc):
                        wait(act, cpT_ps, gc + 1)
                        wait(act, oT_ps, gc)
                        nc.scalar.activation(pcT[:], m1[:], ACT.Copy).then_inc(cpT_sb, 1)
                    if s == 5 and has(g1):
                        wait(act, ctxT_ps, g1 + 1)
                        wait(act, vx_ps, g1)
                        nc.scalar.activation(ctxT[:], m2[:, 0:G * S], ACT.Copy).then_inc(ctxT_sb, 1)
                    if s == 7 and has(g1):
                        wait(act, kxT_ps, g1 + 1)
                        wait(act, xscore_ps, g1)
                        nc.scalar.activation(kxT[:], m2[:, 0:G * S], ACT.Copy, scale=RSQRT_C).then_inc(kxT_sb, 1)
                    if s == 7 and has(g2):
                        wait(act, wT_ps, g2 + 1)
                        wait(act, w_rows_in, 16 * g2)
                        nc.scalar.activation(wT[:], m1[0:E, :], ACT.Copy).then_inc(wT_sb, 1)
                    if s == 9 and has(g2):
                        wait(act, x2T_sb, g2 + 1)
                        wait(act, z_full_done, E * g2)
                        nc.scalar.activation(x2T[:], x2T_next[:], ACT.Copy).then_inc(x2T_moved, 1)
                    if s == 9 and has(g1):
                        wait(act, xmax_done, g1 + 1)
                        wait(act, pxT_ps, g1)
                        wait(act, rsum_x_done, g1)
                        for b in range(G):
                            last = nc.scalar.activation(px[:, b, :], m1[:, b * S:(b + 1) * S], ACT.Exp,
                                                        bias=nmax_x[:, b:b + 1],
                                                        accum_out=sum_x[:, b:b + 1])
                        last.then_inc(xexp_done, 1)
                    if s == 10 and has(g1):
                        wait(act, vx_ps, g1 + 1)
                        wait(act, att_ps, g1)
                        nc.scalar.activation(vx[:], m0[0:S, :], ACT.Copy).then_inc(vx_sb, 1)
                    if s == (12 if has(i) else 11) and has(g1):
                        wait(act, pxT_ps, g1 + 1)
                        nc.scalar.activation(pxT[:], m1[0:S, :], ACT.Copy).then_inc(pxT_sb, 1)
                    for g, e in z_work(i, s):
                        z_high(g, e)
                if isinstance(i, int) and i == NG:
                    end_scale(1, 7)

            passes(act, body)

        @block.vector
        def _(dve):
            def stats(g, src, bn, mv, done):
                plain(dve)
                for b in range(G):
                    last = nc.vector.bn_stats(bn[:, b, :], rows(src, g, b))
                last.then_inc(done, 1)
                wait(dve, done, 2 * g + 1)
                plain(dve)
                for b in range(G):
                    last = nc.vector.bn_aggr(mv[:, b, :], bn[:, b, :])
                last.then_inc(done, 1)

            def setup():
                dve.wait_ge(small_in, 16 * 7)
                nc.vector.tensor_tensor(sim_sq[:], sim_sb[:], sim_sb[:], ALU.mult).then_inc(prep_dve, 1)
                dve.wait_ge(consts, 1)
                nc.vector.tensor_copy(iota_f[:], iota_i[:]).then_inc(prep_dve, 1)
                dve.wait_ge(prep_pe, 3)
                nc.vector.tensor_copy(sim_sq[:], acc_p[V][:, 0:E]).then_inc(prep_dve, 1)

            def weight_max(m):
                dve.wait_ge(proj_in[m], 16)
                nc.vector.tensor_reduce(wmax[:, m:m + 1], stage[:, m].rearrange("p e h -> p (e h)"), AX_X,
                                        ALU.max, apply_absolute_value=True).then_inc(wmax_done, 1)

            def setup_weights():
                dve.wait_ge(nrm_root, 1)
                step = prep_chain
                nc.vector.tensor_scalar(sim_nrm[:], sim_nrm[:], 1e-12, None, ALU.max).then_inc(step, 1)
                dve.wait_ge(step, 1)
                nc.vector.reciprocal(sim_nrm[:], sim_nrm[:]).then_inc(step, 1)
                dve.wait_ge(step, 2)
                nc.vector.tensor_tensor(sn[:], sim_sb[:], sim_nrm[:], ALU.mult).then_inc(prep_dve, 1)
                dve.wait_ge(wmax_shared, 1)
                nc.vector.tensor_scalar(wmax_all[:], wmax_all[:], 2.0 ** -60, 2.0 ** 60, ALU.max,
                                        ALU.min).then_inc(step, 1)
                dve.wait_ge(step, 3)
                nc.vector.tensor_scalar(w_pow[:].bitcast(U32), wmax_all[:].bitcast(U32), 0x7F800000, None,
                                        ALU.bitwise_and).then_inc(step, 1)
                dve.wait_ge(step, 4)
                nc.vector.reciprocal(w_up[:], w_pow[:]).then_inc(step, 1)
                nc.vector.tensor_scalar(score_scale[:], w_pow[:, Q:Q + 1], w_pow[:, K:K + 1], RSQRT_C,
                                        ALU.mult, ALU.mult)
                nc.vector.tensor_scalar(out_scale[:], w_pow[:, V:V + 1], w_pow[:, O:O + 1], 1.0 / W_UP,
                                        ALU.mult, ALU.mult).then_inc(step, 1)
                dve.wait_ge(step, 6)
                nc.vector.tensor_scalar(w_up[:], w_up[:], W_UP, None, ALU.mult).then_inc(prep_dve, 1)
                dve.wait_ge(tanh_done, 1)
                nc.vector.tensor_scalar(out_scale[:], out_scale[:], tanh_f[:], None, ALU.mult).then_inc(prep_dve, 1)

            def weight_low(m):
                dve.wait_ge(hi_done, m + 1)
                nc.vector.scalar_tensor_tensor(
                    out=w_lo[:, m].rearrange("p e h -> p (e h)"), in0=stage[:, m].rearrange("p e h -> p (e h)"),
                    scalar=w_up[:, m:m + 1], in1=w_hi[:, m].rearrange("p e h -> p (e h)"),
                    op0=ALU.mult, op1=ALU.subtract).then_inc(lo_done, 1)

            def gate_logits(g):
                def link(ins, n):
                    ins.then_inc(gate_step, 1)
                    dve.wait_ge(gate_step, GATE_STEPS * g + n)

                wait(dve, logit_ps, g + 1)
                lg = m0[:, 0:G * E].rearrange("p (b e) -> p b e", e=E)
                link(nc.vector.tensor_tensor(logit[:], lg, rnorm2[:].unsqueeze(2).broadcast_to([P, G, E]),
                                             ALU.mult), 1)
                link(nc.vector.tensor_tensor(logit[:], logit[:], sig[:].unsqueeze(1).broadcast_to([P, G, E]),
                                             ALU.subtract), 2)
                plain(dve)
                for b in range(G):
                    last = nc.vector.max(top[:, b, :], logit[:, b, :])
                last.then_inc(gate_step, 1)

            def gate_mask(g):
                def link(ins, n):
                    ins.then_inc(gate_step, 1)
                    dve.wait_ge(gate_step, GATE_STEPS * g + n)

                dve.wait_ge(gate_step, GATE_STEPS * g + 3)
                plain(dve)
                for b in range(G):
                    nc.vector.max_index(top_at[:, b, :], top[:, b, :], logit[:, b, :])
                nc.vector.tensor_scalar(inactive[:], top[:, :, 0], 0.0, None, ALU.is_le)
                link(nc.vector.tensor_scalar(gate_max[:], top[:, :, 0], 0.0, None, ALU.max), 4)
                nc.vector.scalar_tensor_tensor(out=gate_arg[:], in0=logit[:], scalar=0.0,
                                               in1=gate_max[:].unsqueeze(2).broadcast_to([P, G, E]),
                                               op0=ALU.max, op1=ALU.subtract).then_inc(gate_arg_done, 1)
                iota_b = iota_f[:].unsqueeze(1).broadcast_to([P, G, E])
                nc.vector.tensor_tensor(fb0[:], iota_b, top_at[:, :, 0:1].broadcast_to([P, G, E]), ALU.is_equal)
                link(nc.vector.tensor_tensor(fb1[:], iota_b, top_at[:, :, 1:2].broadcast_to([P, G, E]),
                                             ALU.is_equal), 5)
                link(nc.vector.tensor_tensor(fb0[:], fb0[:], fb1[:], ALU.add), 6)
                link(nc.vector.tensor_tensor(fb0[:], fb0[:], inactive[:].unsqueeze(2).broadcast_to([P, G, E]),
                                             ALU.mult), 7)
                link(nc.vector.scalar_tensor_tensor(out=mask[:], in0=logit[:], scalar=0.0, in1=fb0[:],
                                                    op0=ALU.is_gt, op1=ALU.add), EXP_AT)

            def gate_softmax(g):
                def link(ins, n):
                    ins.then_inc(gate_step, 1)
                    dve.wait_ge(gate_step, GATE_STEPS * g + n)

                w_g = w_all[:, bass.ds(G * g, G), :]
                wait(dve, gate_exp, g + 1)
                link(nc.vector.tensor_tensor(mask[:], gate_e[:], mask[:], ALU.mult), EXP_AT + 1)
                link(nc.vector.reduce_sum(wsum[:], mask[:], AX_X), EXP_AT + 2)
                link(nc.vector.reciprocal(wsum[:], wsum[:]), EXP_AT + 3)
                wait(dve, wT_ps, g)
                link(nc.vector.tensor_tensor(w_new[:], mask[:], wsum[:].unsqueeze(2).broadcast_to([P, G, E]),
                                             ALU.mult), EXP_AT + 4)
                plain(dve)
                nc.vector.tensor_copy(w_g, w_new[:]).then_inc(w_ready, 1)

            def z_scale(g, e):
                n = E * g + e
                if e == 0:
                    wait(dve, x2T_moved, g + 1)
                if e % 2 == 0:
                    j = e // 2
                    wait(dve, w_bc_in[j % W_SLOTS], 16 * (E // 2 // W_SLOTS * g + j // W_SLOTS + 1))
                if e >= Z_SLOTS:
                    wait_low(dve, g, e - Z_SLOTS)
                else:
                    wait_low(dve, g - 1, E + e - Z_SLOTS)
                nc.vector.tensor_tensor(z_full[:, e % Z_SLOTS, :], w_bc[:, e // 2 % W_SLOTS, e % 2], x2T[:],
                                        ALU.mult).then_inc(z_full_done, 1)

            def z_low(g, e):
                wait(dve, z_hi_done, E * g + e + 1)
                nc.vector.tensor_tensor(z[:, 1, e, :], z_full[:, e % Z_SLOTS, :], z[:, 0, e, :],
                                        ALU.subtract).then_inc(lo_dve, 1)

            def scale_outputs(g, k):
                b, q = divmod(k, E // 4)
                slot = k % SUM_SLOTS
                wait(dve, y_ps, 4 * G * g + k + 1)
                if k == 0:
                    wait(dve, w_out_done, g + 1)
                if q == 0:
                    wait(dve, sum_step, SUM_STEPS * (G * g + b - 1))
                nc.vector.tensor_tensor(parts[:, slot], y_p[k % 2][:].rearrange("p (e c) -> p e c", e=4),
                                        w_out[:, b, 4 * q:4 * q + 4].unsqueeze(2).broadcast_to([P, 4, P]),
                                        ALU.mult).then_inc(y_scaled, 1)

            def end_outputs(pair, n):
                g, b = END[pair]
                q = n // 2
                slot = END_SLOTS[pair]
                if n % 2 == 0:
                    dve.wait_ge(y_ps, 4 * G * g + 4 * b + n + 1)
                    if n == 0:
                        dve.wait_ge(w_out_done, g + 1)
                        if pair == 1:
                            dve.wait_ge(sum_step, SUM_STEPS * END_SUMMED)
                        elif pair == 2:
                            dve.wait_ge(sum_step, SUM_STEPS * (END_SUMMED + 1))
                    nc.vector.tensor_tensor(parts[:, slot + q], end_p[n % 4][:].rearrange("p (e c) -> p e c", e=4),
                                            end_w[pair][:, b, 4 * q:4 * q + 4].unsqueeze(2).broadcast_to([P, 4, P]),
                                            ALU.mult).then_inc(y_scaled, 1)
                if n in (3, 5, 7):
                    dve.wait_ge(end_scaled, 4 * pair + q + 1)
                    dve.wait_ge(end_step, SUM_STEPS * pair + q - 1)
                    nc.vector.tensor_tensor(parts[:, slot + 4], parts[:, slot + 4], parts[:, slot + 4 + q],
                                            ALU.add).then_inc(end_step, 1)

            def end_rest(pair):
                g, b = END[pair]
                done = SUM_STEPS * pair
                first = END_SLOTS[pair] + 4
                dve.wait_ge(end_step, done + 3)
                nc.vector.tensor_tensor(parts[:, first, 0:2], parts[:, first, 0:2], parts[:, first, 2:4],
                                        ALU.add).then_inc(end_step, 1)
                dve.wait_ge(end_step, done + 4)
                nc.vector.tensor_tensor(parts[:, first, 0], parts[:, first, 0], parts[:, first, 1],
                                        ALU.add).then_inc(end_step, 1)
                dve.wait_ge(end_step, done + 5)
                nc.vector.tensor_tensor(rows(x_all, g, b + 1), rows(x_all, g, b + 1), parts[:, first, 0],
                                        ALU.add).then_inc(end_step, 1)

            def normed(g, dst, mv, rstd, done):
                for b in range(G):
                    last = nc.vector.tensor_scalar(dst[:, b, :], rows(x_all, g, b), mv[:, b, 0:1],
                                                   rstd[:, b:b + 1], ALU.subtract, ALU.mult)
                last.then_inc(done, 1)

            def first_stats(g):
                if isinstance(g, int):
                    dve.wait_ge(x_in[max(c for c, first in enumerate(X_LOADS) if first <= g * G)], 16)
                wait(dve, rstd1_done, 2 * g)
                stats(g, x_all, bn1, mv1, bn1_done)

            def body(i):
                g1, g2, gc, gd = i + 2, i + 1, i - 1, i - 2
                first, second = isinstance(i, int) and i == -2, isinstance(i, int) and i == -1
                end = isinstance(i, int) and i >= NG
                if first:
                    first_stats(0)
                    setup()
                for s in range(E):
                    zs = z_work(i, s)
                    if s == 8 and has(gc):
                        wait(dve, o_hi_done, gc + 1)
                        hi, lo = o_end if end else (o_hi, o_lo)
                        nc.vector.tensor_tensor(lo[:], m0[:], hi[:], ALU.subtract).then_inc(o_lo_done, 1)
                    for g, e in zs[:-1]:
                        z_scale(g, e)
                    if end:
                        for pair, n in end_work(i, s, END_DVE):
                            end_outputs(pair, n)
                            if pair > 0 and n == 2:
                                end_rest(pair - 1)
                    else:
                        if s < 8 and has(gd):
                            scale_outputs(gd, 8 + s)
                        if s >= 9 and has(gc):
                            scale_outputs(gc, s - 9)
                    if s == 2 and has(g1):
                        wait(dve, rstd1_done, 2 * g1 + 2)
                        wait(dve, xnT_ps, g1)
                        normed(g1, xn, mv1, rstd1, xn_done)
                    for g, e in zs[-1:]:
                        z_scale(g, e)
                    if s == 0 and has(g2):
                        wait(dve, rstd2_done, 2 * g2 + 2)
                        wait(dve, x2T_ps, g2)
                        normed(g2, x2, mv2, rstd2, x2_done)
                    if s == 1 and has(gc):
                        wait(dve, cscore_ps, gc + 1)
                        wait(dve, cexp_done, gc)
                        nc.vector.tensor_reduce(nmax_c[:], m1[:].rearrange("p (b t) -> p b t", b=G), AX_X,
                                                ALU.max, negate=True).then_inc(cmax_done, 1)
                        wait(dve, cmax_done, 2 * gc + 1)
                        nc.vector.tensor_scalar(nmax_c[:], nmax_c[:], score_scale[:], None,
                                                ALU.mult).then_inc(cmax_done, 1)
                    if s == 3 and has(g2):
                        wait(dve, norm_step, 2 * g2 + 2)
                        nc.vector.tensor_scalar(rnorm2[:], norm2[:], 1e-12, X_UP, ALU.max,
                                                ALU.mult).then_inc(rnorm_done, 1)
                        wait(dve, rnorm_done, g2 + 1)
                        nc.vector.reciprocal(rnorm2[:], rnorm2[:]).then_inc(rnorm_inv, 1)
                    if s == 4 and has(g2):
                        wait(dve, rnorm_inv, g2 + 1)
                        gate_logits(g2)
                    if s == 5 and has(gc):
                        wait(dve, cexp_done, gc + 1)
                        wait(dve, rs_c_done, gc)
                        nc.vector.reciprocal(rsum_c[:], sum_c[:]).then_inc(rsum_c_done, 1)
                    if s == 5 and has(g2):
                        gate_mask(g2)
                        gate_softmax(g2)
                    if s == 9 and has(g1):
                        wait(dve, xscore_ps, g1 + 1)
                        wait(dve, xexp_done, g1)
                        nc.vector.tensor_reduce(nmax_x[:], m1[:, 0:G * S].rearrange("p (b t) -> p b t", b=G),
                                                AX_X, ALU.max, negate=True).then_inc(xmax_done, 1)
                    if s == 10 and has(g1 + 1):
                        first_stats(g1 + 1)
                    if s == 12 and has(g1):
                        wait(dve, xexp_done, g1 + 1)
                        nc.vector.reciprocal(rsum_x[:], sum_x[:]).then_inc(rsum_x_done, 1)
                    if s == 14 and has(g1):
                        wait(dve, att_ps, g1 + 1)
                        wait(dve, rsum_x_done, g1 + 1)
                        for b in range(G):
                            last = nc.vector.scalar_tensor_tensor(
                                out=rows(x_all, g1, b), in0=m0[:, tok(b)], scalar=rsum_x[:, b:b + 1],
                                in1=rows(x_all, g1, b), op0=ALU.mult, op1=ALU.add)
                        last.then_inc(x1_done, 1)
                    if s == 15 and has(g1):
                        wait(dve, x1_done, g1 + 1)
                        wait(dve, norm_step, 2 * g1)
                        stats(g1, x_all, bn2, mv2, bn2_done)
                    for g, e in zs:
                        if e >= EARLY:
                            z_low(g, e)
                    if s in (2, 3, 10, 12) and first:
                        weight_max((2, 3, 10, 12).index(s))
                    if s == 15 and first:
                        setup_weights()
                    if isinstance(i, int) and (i, s) in LOW_AT:
                        weight_low(LOW_AT.index((i, s)))
                if end:
                    for pair, n in end_work(i, E, END_DVE):
                        end_outputs(pair, n)
                    if i == NG + 1:
                        end_rest(2)
                elif has(gc):
                    scale_outputs(gc, 7)

            passes(dve, body, x_in)

        @block.tensor
        def _(pe):
            pe.wait_ge(small_in, 16 * 7)
            pe.wait_ge(consts, 1)
            nc.tensor.matmul(acc_p[Q][:, 0:P], wk_sb[:], wq_sb[:], start=True, stop=True).then_inc(prep_pe, 1)
            nc.tensor.transpose(acc_p[K][:, 0:P], wv_sb[:], ident[:]).then_inc(prep_pe, 1)
            pe.wait_ge(prep_dve, 1)
            nc.tensor.matmul(acc_p[V][:, 0:E], ones[:], sim_sq[:], start=True, stop=True).then_inc(prep_pe, 1)

            def out_chunk(g, k):
                b, q = divmod(k, E // 4)
                if k == 0:
                    wait(pe, o_lo_done, g + 1)
                    if isinstance(g, int) and g == 0:
                        pe.wait_ge(lo_done, 4)
                wait(pe, y_scaled, 4 * G * g + k - 1)
                for n, (lhs, rhs) in enumerate(((o_hi, w_hi), (o_hi, w_lo), (o_lo, w_hi))):
                    last = nc.tensor.matmul(y_p[k % 2][:], lhs[:, tok(b)],
                                            rhs[:, O, 4 * q:4 * q + 4, :].rearrange("p e h -> p (e h)"),
                                            start=(n == 0), stop=(n == 2))
                last.then_inc(y_ps, 1)

            def end_chunk(pair, n):
                g, b = END[pair]
                q = n // 2
                if b == 0 and n == 0:
                    pe.wait_ge(o_lo_done, g + 1)
                if pair == 0 and n < 2:
                    pe.wait_ge(y_scaled, END_SCALED - 1 + n)
                elif pair == 0 and n < 4:
                    pe.wait_ge(acc_sb[Q if n == 2 else K], NG)
                elif n % 2 == 0:
                    pe.wait_ge(y_scaled, END_SCALED + 4 * pair + q - 1)
                else:
                    pe.wait_ge(end_scaled, 4 * pair + q - 1)
                hi, lo = (o_hi, o_lo) if pair == 0 else o_end
                for m, (lhs, rhs) in enumerate(((hi, w_hi), (hi, w_lo), (lo, w_hi))):
                    last = nc.tensor.matmul(end_p[n % 4][:], lhs[:, tok(b + n % 2)],
                                            rhs[:, O, 4 * q:4 * q + 4, :].rearrange("p e h -> p (e h)"),
                                            start=(m == 0), stop=(m == 2))
                last.then_inc(y_ps, 1)

            SMALL_AT = [(Q, 1), (K, 0), (K, 2), (V, 1)]

            def small_product(i, s, b):
                g1, g2 = i + 2, i + 1
                if s == 4 and has(g2):
                    if b == 0:
                        if isinstance(i, int) and i == -1:
                            pe.wait_ge(prep_dve, 4)
                        wait(pe, x2T_sb, g2 + 1)
                    last = nc.tensor.matmul(m0[:, b * E:(b + 1) * E], x2T_next[:, tok(b)], sn[:],
                                            start=True, stop=True)
                    if b == G - 1:
                        last.then_inc(logit_ps, 1)
                if s == 9 and has(g1):
                    if b == 0:
                        wait(pe, xnT_sb, g1 + 1)
                        wait(pe, kxT_sb, g1 + 1)
                        wait(pe, wT_sb, cap(i + 2))
                    last = nc.tensor.matmul(m1[:, b * S:(b + 1) * S], xnT[:, tok(b)],
                                            kxT[:, b * S:(b + 1) * S], start=True, stop=True)
                    if b == G - 1:
                        last.then_inc(xscore_ps, 1)

            def body(i):
                g1, g2, gc, gd = i + 2, i + 1, i - 1, i - 2
                end = isinstance(i, int) and i >= NG
                for s in range(E):
                    zs = z_work(i, s)
                    if has(i):
                        if isinstance(i, int) and i == 0 and s == 0:
                            pe.wait_ge(lo_done, 3)
                        wait_low(pe, i, s)
                        for m in (Q, K, V):
                            if s == 0:
                                wait(pe, acc_sb[m], i)
                            for n, (w, half) in enumerate(((w_hi, 0), (w_lo, 0), (w_hi, 1))):
                                last = nc.tensor.matmul(acc_p[m][:], w[:, m, s, :], z[:, half, s, :],
                                                        start=(s == 0 and n == 0), stop=(s == E - 1 and n == 2))
                                if (m, n) in SMALL_AT:
                                    small_product(i, s, SMALL_AT.index((m, n)))
                            if s == E - 1:
                                last.then_inc(acc_ps[m], 1)
                        if s < E - 1:
                            last.then_inc(expert_used, 1)
                        else:
                            pe.sem_inc(expert_used, 1)
                    else:
                        for b in range(G):
                            small_product(i, s, b)
                    if end:
                        for pair, n in end_work(i, s, END_PE):
                            end_chunk(pair, n)
                    else:
                        if s < 8 and has(gd):
                            out_chunk(gd, 8 + s)
                        if s >= 9 and has(gc):
                            out_chunk(gc, s - 9)
                    if s == 0 and has(gc):
                        wait(pe, acc_sb[V], gc + 1)
                        wait(pe, x1_done, cap(i + 2))
                        if isinstance(i, int):
                            wait(pe, o_lo_done, gc)
                        for b in range(G):
                            last = nc.tensor.transpose(m0[:, tok(b)], vT[:, tok(b)], ident[:])
                        last.then_inc(v_ps, 1)
                    if s == 1 and has(gc):
                        wait(pe, acc_sb[K], gc + 1)
                        wait(pe, pxT_sb, cap(i + 2))
                        for b in range(G):
                            last = nc.tensor.matmul(m1[:, tok(b)], qT[:, tok(b)], kT[:, tok(b)],
                                                    start=True, stop=True)
                        last.then_inc(cscore_ps, 1)
                    if s == 2 and has(g2):
                        wait(pe, x2_done, g2 + 1)
                        wait(pe, v_tok_sb, cap(i))
                        for b in range(G):
                            last = nc.tensor.transpose(m0[:, tok(b)], x2[:, b, :], ident[:])
                        last.then_inc(x2T_ps, 1)
                    if s == 3 and has(g1):
                        wait(pe, xn_done, g1 + 1)
                        wait(pe, cexp_done, cap(i))
                        for b in range(G):
                            last = nc.tensor.transpose(m1[:, tok(b)], xn[:, b, :], ident[:])
                        last.then_inc(xnT_ps, 1)
                    if s == 5 and has(gc):
                        wait(pe, cexp_done, gc + 1)
                        wait(pe, xnT_sb, cap(i + 3))
                        for b in range(G):
                            last = nc.tensor.transpose(m1[:, tok(b)], pc[:, b, :], ident[:])
                        last.then_inc(cpT_ps, 1)
                    if s == 4 and has(g1):
                        wait(pe, ctx_loaded, 16 * g1 + 16)
                        wait(pe, kxT_sb, g1)
                        for b in range(G):
                            last = nc.tensor.transpose(m2[:, b * S:(b + 1) * S], ctx_g[:, b, :],
                                                       ident[0:S, 0:S])
                        last.then_inc(ctxT_ps, 1)
                    if s == 7 and has(g1):
                        if isinstance(i, int) and i == -2:
                            pe.wait_ge(tanh_done, 2)
                        wait(pe, ctxT_sb, g1 + 1)
                        nc.tensor.matmul(m2[:, 0:G * S], m_kq[:], ctxT[:], start=True, stop=True).then_inc(kxT_ps, 1)
                    if s == 7 and has(g2):
                        wait(pe, w_ready, g2 + 1)
                        wait(pe, cpT_sb, cap(i))
                        if isinstance(i, int):
                            wait(pe, xnT_sb, cap(i + 3))
                        for b in range(G):
                            last = nc.tensor.transpose(m1[0:E, tok(b)], w_new[:, b, :], ident[:])
                        last.then_inc(wT_ps, 1)
                    if s == 7 and has(gc):
                        wait(pe, v_tok_sb, gc + 1)
                        wait(pe, cpT_sb, gc + 1)
                        wait(pe, gate_step, GATE_STEPS * (cap(i + 2) - 1) + 1)
                        for b in range(G):
                            last = nc.tensor.matmul(m0[:, tok(b)], v_sb[:, b, :], pcT[:, tok(b)],
                                                    start=True, stop=True)
                        last.then_inc(oT_ps, 1)
                    if s == 10 and has(g1):
                        wait(pe, o_lo_done, cap(i))
                        for b in range(G):
                            last = nc.tensor.matmul(m0[0:S, tok(b)], ctxT[:, b * S:(b + 1) * S], wvT[:],
                                                    start=True, stop=True)
                        last.then_inc(vx_ps, 1)
                    if s == 12 and has(g1):
                        wait(pe, xexp_done, g1 + 1)
                        for b in range(G):
                            last = nc.tensor.transpose(m1[0:S, tok(b)], px[:, b, :], ident[:])
                        last.then_inc(pxT_ps, 1)
                    if s == 14 and has(g1):
                        wait(pe, pxT_sb, g1 + 1)
                        wait(pe, vx_sb, g1 + 1)
                        for b in range(G):
                            last = nc.tensor.matmul(m0[:, tok(b)], pxT[:, tok(b)], vx[:, tok(b)],
                                                    start=True, stop=True)
                        last.then_inc(att_ps, 1)
                if end:
                    for pair, n in end_work(i, E, END_PE):
                        end_chunk(pair, n)
                elif has(gc):
                    out_chunk(gc, 7)

            passes(pe, body)


_INS = ['x', 'ctx_1024', 'g_xattn', 'g_ffn', 'L0_xattn_Wk', 'L0_xattn_Wq', 'L0_xattn_Wv', 'L0_ffn_sim_matrix',
        'L0_ffn_gates', 'L0_ffn_q_proj', 'L0_ffn_k_proj', 'L0_ffn_v_proj', 'L0_ffn_o_proj']


def kernel(**inputs):
    import numpy as _np
    import concourse.bacc as _bacc
    from concourse import mybir as _mybir
    from concourse.bass_utils import run_bass_kernel_spmd as _run

    nc = _bacc.Bacc("TRN2", target_bir_lowering=False, num_devices=1)
    arrays, args = {}, []
    for name in _INS:
        a = _np.ascontiguousarray(inputs[name])
        arrays[f"in_{name}_dram"] = a
        args.append(nc.dram_tensor(f"in_{name}_dram", a.shape, _mybir.dt.from_np(a.dtype), kind="ExternalInput").ap())
    out = nc.dram_tensor("out_dram", arrays["in_x_dram"].shape, _mybir.dt.float32, kind="ExternalOutput").ap()
    flamingo_gated_moe_attention(nc, *args, out)
    r = _run(nc, [arrays], core_ids=[0])
    return r.results[0]["out_dram"]
```
